# Optimizing a Trainium2 kernel written in Bass

```python
import numpy as np
import jax
import jax.numpy as jnp

def _softmax(x, axis=-1):
    return jax.nn.softmax(x, axis=axis)

def _gelu(x):
    return jax.nn.gelu(x, approximate=True)

def _silu(x):
    return jax.nn.silu(x)

def _sigmoid(x):
    return jax.nn.sigmoid(x)

def _layernorm(x, axis=-1, eps=1e-05):
    m = jnp.mean(x, axis=axis, keepdims=True)
    v = jnp.var(x, axis=axis, keepdims=True)
    return (x - m) / jnp.sqrt(v + eps)

def _scatter_add(tgt, idx, src, axis=0):
    return tgt.at[idx].add(src)

def _segment_sum(src, seg, n):
    return jax.ops.segment_sum(src, seg, n)
kernel_name = 'mk_xattn_ffn_d1_seqx_r2_393e41'

def setup_inputs(seed: int=0):
    np.random.seed(seed)
    _w = jnp.asarray

    def _rec_inputs():
        import jax
        import jax.numpy as jnp
        _rk = jax.random.key(seed)
        x = -0.0003929 + 0.9999 * jax.random.normal(jax.random.fold_in(_rk, 1), (32, 512, 512), jnp.float32)
        _lenS = 512 - jax.random.randint(jax.random.fold_in(_rk, 7), (32,), 0, max(1, 512 // 4) + 1, jnp.int32)
        _lenS2 = 512 - jax.random.randint(jax.random.fold_in(_rk, 8), (32,), 0, max(1, 512 // 4) + 1, jnp.int32)
        _ctx_1024P = jax.random.normal(jax.random.fold_in(_rk, 11), (32, 16, 512), jnp.float32)
        _ctx_1024c = jax.random.dirichlet(jax.random.fold_in(_rk, 511), 0.3 * jnp.ones((16,), jnp.float32), (32, 512))
        _ctx_1024t = jnp.einsum('bsk,bkd->bsd', _ctx_1024c, _ctx_1024P)
        _ctx_1024t = _ctx_1024t * jax.lax.rsqrt(jnp.mean(jnp.square(_ctx_1024t)) + 1e-12) * 0.953939
        ctx_1024 = -1.52775e-05 + 0.999936 * (_ctx_1024t + 0.3 * jax.random.normal(jax.random.fold_in(_rk, 611), (32, 512, 512), jnp.float32))
        return (x, ctx_1024)
    x, ctx_1024 = _rec_inputs()

    def _L0_xattn_setup():
        import jax, jax.numpy as jnp
        import numpy as np
        DIM = 512
        key = jax.random.key(seed)
        k1, k2, k3, k4 = jax.random.split(key, 4)
        decoder_states = jax.random.normal(k1, (32, 256, DIM), dtype=jnp.float32)
        encoder_states = jax.random.normal(k2, (32, 512, DIM), dtype=jnp.float32)
        bound = 1.0 / np.sqrt(2 * DIM)
        mlp_weight = jax.random.uniform(k3, (1, 2 * DIM), minval=-bound, maxval=bound, dtype=jnp.float32)
        mlp_bias = jax.random.uniform(k4, (1,), minval=-bound, maxval=bound, dtype=jnp.float32)
        return {'decoder_states': decoder_states, 'encoder_states': encoder_states, 'step': 0, 'mlp_weight': mlp_weight, 'mlp_bias': mlp_bias}
    _L0_xattn_all = _L0_xattn_setup()
    _L0_xattn_in = {k: v for k, v in _L0_xattn_all.items() if k in ('mlp_weight', 'mlp_bias')}
    del _L0_xattn_all

    def _L0_ffn_setup():
        import jax, jax.numpy as jnp
        import numpy as np
        B, S, H, E = (2, 4096, 512, 8)
        SCALE = 0.5
        key = jax.random.key(seed)
        k1, k2 = jax.random.split(key)
        x = jax.random.normal(k1, (B, S, H), dtype=jnp.float32)
        gate_w = jax.random.normal(k2, (E, H), dtype=jnp.float32) * 0.02
        coeff = SCALE * (1.0 + 0.05 * jnp.arange(E, dtype=jnp.float32))
        expert_w = coeff[:, None, None] * jnp.eye(H, dtype=jnp.float32)
        return {'x': x, 'gate_w': gate_w, 'expert_w': expert_w}
    _L0_ffn_all = _L0_ffn_setup()
    _L0_ffn_in = {k: v for k, v in _L0_ffn_all.items() if k in ('gate_w', 'expert_w')}
    del _L0_ffn_all
    return {'x': x, 'ctx_1024': ctx_1024, 'L0_xattn_mlp_weight': _L0_xattn_in['mlp_weight'], 'L0_xattn_mlp_bias': _L0_xattn_in['mlp_bias'], 'L0_ffn_gate_w': _L0_ffn_in['gate_w'], 'L0_ffn_expert_w': _L0_ffn_in['expert_w']}

def reference(x, ctx_1024, L0_xattn_mlp_weight, L0_xattn_mlp_bias, L0_ffn_gate_w, L0_ffn_expert_w):
    import jax
    import jax.numpy as jnp

    def _L0_xattn_ref(decoder_states, encoder_states, step, mlp_weight, mlp_bias):
        import jax, jax.numpy as jnp
        import numpy as np
        DIM = 512
        w = mlp_weight[0]
        w_enc, w_dec = (w[:DIM], w[DIM:])
        enc_proj = encoder_states @ w_enc
        dec_proj = decoder_states @ w_dec
        attn = dec_proj[:, :, None] + enc_proj[:, None, :] + mlp_bias[0]
        return attn

    def _L0_ffn_ref(x, gate_w, expert_w):
        import jax, jax.numpy as jnp
        import numpy as np
        B, S, H, E = (2, 4096, 512, 8)
        SCALE = 0.5
        scores = jnp.einsum('bsh,eh->bse', x, gate_w)
        chosen = jnp.argmax(scores, axis=-1)
        onehot = jax.nn.one_hot(chosen, gate_w.shape[0], dtype=x.dtype)
        expert_out = jnp.einsum('bsh,efh->bsef', x, expert_w)
        return x + jnp.einsum('bsef,bse->bsf', expert_out, onehot)
    x = x + _L0_xattn_ref(_layernorm(x, axis=-1), ctx_1024, 0, L0_xattn_mlp_weight, L0_xattn_mlp_bias)
    x = x + _L0_ffn_ref(_layernorm(x, axis=-1), L0_ffn_gate_w, L0_ffn_expert_w)
    return x

_drawn_inputs = setup_inputs


def setup_inputs(seed=0):
    import zlib

    import numpy as np

    out = dict(_drawn_inputs(seed))
    spreads = {}
    factors = {}
    for name, (base, spread) in spreads.items():
        noise = np.random.default_rng([zlib.crc32(name.encode()), seed]).standard_normal(out[name].shape)
        drawn = base * np.exp(spread * noise) if base else spread * noise
        out[name] = jnp.asarray(drawn.astype(out[name].dtype))
    for name, factor in factors.items():
        out[name] = (out[name] * factor).astype(out[name].dtype)
    return out
```

```python
import concourse.bass as bass
from concourse import mybir
from contextlib import ExitStack
import numpy as np

FP32 = mybir.dt.float32
FP16 = mybir.dt.float16
BF16 = mybir.dt.bfloat16
I32 = mybir.dt.int32
U32 = mybir.dt.uint32
ALU = mybir.AluOpType
ACT = mybir.ActivationFunctionType
AX = mybir.AxisListType

P = 128
B, S, H, E = 32, 512, 512, 8
N = B * S
HC = H // P
TS = 8
STEP_TOKENS = TS * P
NS = N // STEP_TOKENS
NG = (N + E * (P - 1)) // P // TS + 1
QUEUE = N + P
DUMMY = E * QUEUE
ENTRIES = DUMMY + TS * P
NO_TOKEN = 1 << 20
EPS = 1e-5
W_TOP = 13
LN_SHIFT = 8
assert ENTRIES % P == 0



def constants():
    p = np.arange(P)[:, None]
    e = np.arange(E)
    j = np.arange(TS)
    c = np.arange(P)
    parts = {
        "ident": (c[None] == p),
        "before": (p < c[None]),
        "batch_of_col": np.where(c < 3 * B, c % B, -1)[None],
        "one_at_31": (np.arange(64) == 31)[None],
        "up_to": np.tril(np.ones((E, E))).reshape(1, -1),
        "first_key": (E - e)[None],
        "expert": e[None],
        "pick": j[None],
        "queue_start": (e * QUEUE)[None],
        "floor_add": (-e * QUEUE)[None],
        "ceil_add": (P - 1 - e * QUEUE)[None],
        "queue_from_dummy": (e * QUEUE - DUMMY)[None],
        "pick_entry": (j * P + DUMMY)[None],
        "first_ids": j[None] * P + p,
    }
    at, cols, out = 0, {}, []
    for name, a in parts.items():
        a = np.broadcast_to(np.asarray(a, np.float32), (P, np.asarray(a).shape[1]))
        cols[name] = (at, at + a.shape[1])
        at += a.shape[1]
        out.append(a)
    return np.ascontiguousarray(np.concatenate(out, 1)), cols


ROUTE = ["scores_copied", "enc_copied", "stat_diff", "stat_sum", "enc_hi", "enc_rest", "enc_mid",
         "enc_parts", "enc_rows0", "enc_rows1", "stat_diff2", "var4", "scores", "best", "is_best",
         "key", "best_key", "onehot", "rstd", "d_scaled", "enc_table", "payload_d", "payload",
         "next_ids", "rank", "rank_own", "counts", "entry_f", "entry"]
PICK = ["full_i", "full", "avail", "prefix_terms", "prefix", "passed", "start0", "expert_f", "start1",
        "chosen", "start_terms", "start_f", "entry", "expert", "taken", "done", "scale_terms", "scale"]
STATS = ["rstd", "ln_scale", "ln_bias", "base_scale", "base_bias"]
KEEP = ["ids_out", "ids_mix"]


def build(nc, x, ctx, mlp_weight, mlp_bias, gate_w, expert_w, const, cols, out):
    x_rows = x.rearrange("b s h -> (b s) h")
    out_rows = out.rearrange("b s h -> (b s) h")
    queue = nc.dram_tensor("queue", [ENTRIES, 2], I32, kind="Internal").ap()

    with ExitStack() as stack:
        def sb(name, shape, dt):
            return stack.enter_context(nc.sbuf_tensor(name, shape, dt))

        def pb(name, shape, dt):
            return stack.enter_context(nc.psum_tensor(name, shape, dt))

        def sem(name):
            return stack.enter_context(nc.semaphore(name))

        cst = sb("cst", [P, const.shape[1]], FP32)

        def table(name):
            return cst[:, cols[name][0]:cols[name][1]]
        ident_b = sb("ident_b", [P, P], BF16)
        before_b = sb("before_b", [P, P], BF16)
        ones_b = sb("ones_b", [P, P], BF16)
        one31_b = sb("one31_b", [P, 64], BF16)
        w_hi = sb("w_hi", [P, E, HC * H], FP16)
        w_lo = sb("w_lo", [P, E, HC * H], FP16)
        w_enc = sb("w_enc", [P, H], FP32)
        bias = sb("bias", [P, 1], FP32)
        eps = sb("eps", [P, 1], FP32)
        g_rows = sb("g_rows", [P, H], FP32)
        g_sum = sb("g_sum", [P, 1], FP32)
        gates = sb("gates", [P, HC, E + 1], FP32)
        w_max = sb("w_max", [P, E], FP32)
        w_amax = sb("w_amax", [P, E], FP32)
        w_exp = sb("w_exp", [P, E], I32)
        w_exp2 = sb("w_exp2", [P, E], I32)
        w_scale = sb("w_scale", [P, E], I32)
        w_unscale = sb("w_unscale", [P, E], I32)
        x_in = sb("x_in", [P, TS, H], FP32)
        c_in = sb("c_in", [P, TS, H], FP32)
        xT = sb("xT", [P, 2, HC * P], FP32)
        junk_a = sb("junk_a", [P, H], FP32)
        enc_col = sb("enc_col", [P, TS], FP32)
        bn = sb("bn", [P, TS, 6], FP32)
        sc = sb("sc", [P, TS, E + 1], FP32)
        enc_now = sb("enc_now", [P, TS], FP32)
        enc_parts = sb("enc_parts", [P, TS, 4], BF16)
        enc_rest = sb("enc_rest", [P, TS], FP32)
        enc_lhs = sb("enc_lhs", [P, TS, 4, B], BF16)
        enc_tab = sb("enc_tab", [P, H], BF16)
        st_diff = sb("st_diff", [P, TS], FP32)
        st_diff2 = sb("st_diff2", [P, TS], FP32)
        st_sum = sb("st_sum", [P, TS], FP32)
        st_var4 = sb("st_var4", [P, TS], FP32)
        st_std = sb("st_std", [P, TS], FP32)
        st_rstd = sb("st_rstd", [P, TS], FP32)
        st_d = sb("st_d", [P, TS], FP32)
        full_sc = sb("full_sc", [P, TS, E], FP32)
        best = sb("best", [P, TS], FP32)
        is_best = sb("is_best", [P, TS, E], FP32)
        key = sb("key", [P, TS, E], FP32)
        best_key = sb("best_key", [P, TS], FP32)
        onehot_pad = sb("onehot_pad", [P, 2 * TS + 1, E], BF16)
        onehot = onehot_pad[:, TS:2 * TS, :]
        counts = sb("counts", [P, E], FP32)
        rank = sb("rank", [P, TS, E], FP32)
        rank_own = sb("rank_own", [P, TS, E], FP32)
        entry_f = sb("entry_f", [P, TS], FP32)
        entry = sb("entry", [P, TS], U32)
        next_ids = sb("next_ids", [P, TS], FP32)
        payload = sb("payload", [P, TS, 2], I32)
        full_i = sb("full_i", [P, E], I32)
        full = sb("full", [P, E], I32)
        avail = sb("avail", [P, E], FP32)
        done = sb("done", [P, E], FP32)
        pre_t = sb("pre_t", [P, E, E], FP32)
        prefix = sb("prefix", [P, E], FP32)
        passed = sb("passed", [P, TS, E], FP32)
        expert_f = sb("expert_f", [P, TS], FP32)
        chosen = sb("chosen", [P, TS, E], FP32)
        start0 = sb("start0", [P, E], FP32)
        start1 = sb("start1", [P, E], FP32)
        start_t = sb("start_t", [P, TS, E], FP32)
        start_f = sb("start_f", [P, TS], FP32)
        taken = sb("taken", [P, E], FP32)
        scale_t = sb("scale_t", [P, TS, E], FP32)
        pick_entry = sb("pick_entry", [P, NG * TS], I32)
        pick_expert = sb("pick_expert", [P, NG * TS], I32)
        pick_scale = sb("pick_scale", [P, NG * TS], FP32)
        meta = sb("meta", [P, TS, 2], I32)
        batch_no = sb("batch_no", [P, TS], I32)
        oh = sb("oh", [P, TS // 2, P], BF16)
        ohT = sb("ohT", [P, TS, P], BF16)
        x_got = sb("x_got", [P, TS, H], FP32)
        x1 = sb("x1", [P, TS, H], FP32)
        x1_sum = sb("x1_sum", [P, TS], FP32)
        x1_nmean = sb("x1_nmean", [P, TS], FP32)
        x1_ss = sb("x1_ss", [P, TS], FP32)
        x1_std = sb("x1_std", [P, TS], FP32)
        x1_rstd = sb("x1_rstd", [P, TS], FP32)
        ln_scale = sb("ln_scale", [P, TS], FP32)
        ln_bias = sb("ln_bias", [P, TS], FP32)
        base_scale = sb("base_scale", [P, TS], FP32)
        base_bias = sb("base_bias", [P, TS], FP32)
        ids_mix = sb("ids_mix", [P, TS], U32)
        ids_out = sb("ids_out", [P, TS], U32)
        ln2 = sb("ln2", [P, 2, H], FP32)
        hiT = sb("hiT", [P, 2, HC * P], FP16)
        loT = sb("loT", [P, 2, HC * P], FP16)
        base = sb("base", [P, 4, H], FP32)
        res = sb("res", [P, 4, H], FP32)

        ps_xT = pb("ps_xT", [P, HC * P], FP32)
        ps_scores = pb("ps_scores", [P, 512], FP32)
        ps_rows = pb("ps_rows", [P, 512], FP32)
        ps_route = pb("ps_route", [P, 512], FP32)
        ps_bcast = pb("ps_bcast", [P, H], FP32)
        ps_lnT = pb("ps_lnT", [P, HC * P], FP32)
        ps_mm = pb("ps_mm", [P, 2, H], FP32)
        ps_sc = ps_scores[:, 0:TS * (E + 1)].rearrange("p (t e) -> p t e", e=E + 1)
        ps_enc = ps_rows[:, 0:H]
        ps_ohT = ps_rows[:, 0:4 * P // 2].bitcast(BF16).rearrange("p (t c) -> p t c", c=P)
        ps_es = ps_route[:, 0:2 * E].rearrange("p (b e) -> p b e", e=E)
        ps_rank = ps_route[:, 128:128 + (TS + 1) * E].rearrange("p (t e) -> p t e", e=E)

        const_in = sem("const_in")
        small_in = sem("small_in")
        gate_in = sem("gate_in")
        queue_fill = sem("queue_fill")
        queue_filled = sem("queue_filled")
        tables_set = sem("tables_set")
        rows_clear = sem("rows_clear")
        gate_chain = sem("gate_chain")
        gate_T = sem("gate_T")
        w_in = [sem(f"w_in{k}") for k in range(2)]
        w_maxed = sem("w_maxed")
        w_allmax = sem("w_allmax")
        w_chain = sem("w_chain")
        w_T = sem("w_T")
        w_hi_set = sem("w_hi_set")
        w_lo_set = sem("w_lo_set")
        got_clear = sem("got_clear")
        x_loaded = [sem(f"x_loaded{k}") for k in range(2)]
        c_loaded = [sem(f"c_loaded{k}") for k in range(2)]
        x_T = sem("x_T")
        x_T_copied = sem("x_T_copied")
        scored = sem("scored")
        ctx_dotted = sem("ctx_dotted")
        x_stats = sem("x_stats")
        route = sem("route")
        enc_scored = sem("enc_scored")
        enc_rowed = sem("enc_rowed")
        ranked = sem("ranked")
        std1_set = sem("std1_set")
        queued = sem("queued")
        pool_waited = sem("pool_waited")
        sp_waited = sem("sp_waited")
        pick = sem("pick")
        meta_in = [sem(f"meta_in{j}") for j in range(TS)]
        got = [sem(f"got{j}") for j in range(TS)]
        keep = sem("keep")
        batch_set = sem("batch_set")
        oh_set = sem("oh_set")
        oh_T = sem("oh_T")
        oh_T_copied = sem("oh_T_copied")
        enc_bcast = sem("enc_bcast")
        x1_set = sem("x1_set")
        nmean_set = sem("nmean_set")
        squared = sem("squared")
        std2_set = sem("std2_set")
        stats = sem("stats")
        ln2_set = sem("ln2_set")
        ln_T = sem("ln_T")
        hi_set = sem("hi_set")
        lo_set = sem("lo_set")
        base_set = sem("base_set")
        multiplied = sem("multiplied")
        res_set = sem("res_set")
        stored = [sem(f"stored{k}") for k in range(4)]

        def route_at(s, name):
            return s * len(ROUTE) + (ROUTE.index(name) + 1)

        def pick_at(g, name):
            return g * len(PICK) + (PICK.index(name) + 1)

        def half_at(chain, g, h, name):
            return (2 * g + h) * len(chain) + (chain.index(name) + 1)

        def tile_no(g, j):
            return g * TS + j

        def on(k, count):
            return not isinstance(k, int) or 0 <= k < count

        def later(k):
            return not isinstance(k, int) or k > 0

        block = stack.enter_context(nc.Block())

        @block.sync
        def _(sp):
            sp.dma_start(cst[:, :], const).then_inc(const_in, 16)
            sp.wait_ge(rows_clear, 1)
            sp.dma_start(g_rows[0:E, :], gate_w).then_inc(gate_in, 16)
            sp.dma_start(g_rows[E:E + 1, :], mlp_weight[:, H:2 * H]).then_inc(gate_in, 16)
            sp.dma_start(w_enc[:, :], mlp_weight[:, 0:H].partition_broadcast(P)).then_inc(small_in, 16)
            sp.dma_start(bias[:, :], mlp_bias.partition_broadcast(P)).then_inc(small_in, 16)
            sp.wait_ge(queue_fill, 1)
            sp.dma_start(queue.rearrange("(p n) c -> p (n c)", p=P),
                         x1[:, :, :].rearrange("p t h -> p (t h)").bitcast(I32)[:, 0:2 * ENTRIES // P])\
              .then_inc(queue_filled, 16)

            def alone(semaphore, value):
                sp.wait_ge(semaphore, value)
                sp.sem_inc(sp_waited, 1)

            def load_half(s, h):
                if later(s):
                    alone(x_T, tile_no(s - 1, 4 * h + 4))
                    alone(x_stats, tile_no(s - 1, 4 * h + 4))
                    alone(ctx_dotted, tile_no(s - 1, 4 * h + 4))
                src = 2 * s + h
                for dst, dram, arrived in ((x_in, x, x_loaded[h]), (c_in, ctx, c_loaded[h])):
                    sp.dma_start(dst[:, 4 * h:4 * h + 4, :],
                                 dram[bass.ds(src, 1), :, :].rearrange("a (j p) h -> p (a j) h", p=P))\
                      .then_inc(arrived, 16)

            for h in range(2):
                load_half(0, h)
            for e in range(E):
                if e >= 2:
                    alone(w_lo_set, HC * (e - 1))
                if e == 1:
                    alone(queue_filled, 16)
                stage = (x_got, x1)[e % 2]
                sp.dma_start(stage[:, 0:HC, :], expert_w[e].rearrange("(c p) h -> p c h", p=P))\
                  .then_inc(w_in[e % 2], 16)

            def step(t):
                s, g = t, t - 2
                if on(s + 1, NS):
                    load_half(s + 1, 0)
                if on(g, NG):
                    alone(pick, pick_at(g, "entry"))
                    routed = g + 1 if not isinstance(g, int) else min(g + 1, NS - 1)
                    alone(queued, 16 * TS * (routed + 1))
                    for j in range(TS):
                        if later(g):
                            alone(x1_set, tile_no(g - 1, j + 1))
                            alone(keep, half_at(KEEP, g - 1, j // 4, "ids_mix"))
                            alone(got[j], 16 * g)
                        at = sp.value_load(pick_entry[0:1, bass.ds(tile_no(g, j), 1)],
                                           min_val=0, max_val=ENTRIES - P)
                        sp.dma_start(meta[:, j, :], queue[bass.ds(at, P), :]).then_inc(meta_in[j], 16)
                if on(s + 1, NS):
                    load_half(s + 1, 1)

            for t in range(5):
                step(t)
            with sp.Fori(5, NS - 1) as t:
                step(t)
            for t in range(NS - 1, NG + 4):
                step(t)
            for k in range(4):
                sp.wait_ge(stored[k], 16 * (NG * TS // 4))

        @block.gpsimd
        def _(pool):
            nc.gpsimd.memset(x1[:, :, :].rearrange("p t h -> p (t h)").bitcast(I32)[:, 0:2 * ENTRIES // P],
                             NO_TOKEN).then_inc(queue_fill, 1)
            for e in range(E):
                pool.wait_ge(w_maxed, e + 1)
                nc.gpsimd.partition_all_reduce(w_amax[:, e:e + 1], w_max[:, e:e + 1], P,
                                               bass.bass_isa.ReduceOp.absmax).then_inc(w_allmax, 1)
            pool.wait_ge(w_lo_set, HC * (E - 1))
            nc.gpsimd.memset(x_got[:, :, :], 0.0).then_inc(got_clear, 1)
            pool.wait_ge(got_clear, 1)
            pool.wait_ge(queue_filled, 16)

            def plain(value, semaphore):
                pool.wait_ge(semaphore, value)
                pool.sem_inc(pool_waited, 1)

            def enqueue(s, j):
                plain(route_at(s, "entry"), route)
                pool.indirect_dma_start(queue, bass.IndirectOffsetOnAxis(ap=entry[:, j:j + 1], axis=0),
                                        payload[:, j, :], None,
                                        bounds_check=ENTRIES - 1, oob_is_err=False).then_inc(queued, 16)

            def gather(g, j):
                if later(g):
                    plain(tile_no(g - 1, j + 1), x1_set)
                plain(16 * (g + 1), meta_in[j])
                pool.indirect_dma_start(x_got[:, j, :], None, x_rows,
                                        bass.IndirectOffsetOnAxis(ap=meta[:, j, 0:1].bitcast(U32), axis=0),
                                        bounds_check=N - 1, oob_is_err=False).then_inc(got[j], 16)

            def scatter(g, j):
                plain(half_at(KEEP, g + 1, j // 4, "ids_out"), keep)
                plain(tile_no(g, j + 1), res_set)
                pool.indirect_dma_start(out_rows, bass.IndirectOffsetOnAxis(ap=ids_out[:, j:j + 1], axis=0),
                                        res[:, j % 4, :], None,
                                        bounds_check=N - 1, oob_is_err=False).then_inc(stored[j % 4], 16)

            gathers = {5: (0, 1, 2), 6: (3, 4), 7: (5, 6)}

            def step(t):
                for i in range(TS):
                    if i == 0 and on(t - 3, NG):
                        gather(t - 3, 7)
                    if i == 0 and on(t - 5, NG):
                        scatter(t - 5, 7)
                    if i > 0 and on(t - 4, NG):
                        scatter(t - 4, i - 1)
                    if i == 4 and on(t - 1, NS):
                        for j in range(TS):
                            enqueue(t - 1, j)
                    if on(t - 2, NG):
                        for j in gathers.get(i, ()):
                            gather(t - 2, j)

            for t in range(5):
                step(t)
            with pool.Fori(5, NS) as t:
                step(t)
            for t in range(NS, NG + 4):
                step(t)
            scatter(NG - 1, 7)

        @block.scalar
        def _(act):
            act.wait_ge(tables_set, 1)
            for e in range(E):
                for c in range(HC):
                    act.wait_ge(w_T, HC * e + c + 1)
                    act.wait_ge(w_chain, 6 * (e + 1))
                    nc.scalar.activation(w_hi[:, e, c * H:(c + 1) * H], ps_mm[:, c % 2, :], ACT.Copy,
                                         scale=w_scale[:, e:e + 1].bitcast(FP32)).then_inc(w_hi_set, 1)

            def std_x1(g, h):
                act.wait_ge(squared, tile_no(g, 4 * h + 4))
                if later(g):
                    act.wait_ge(stats, half_at(STATS, g - 1, h, "rstd"))
                nc.scalar.activation(x1_std[:, 4 * h:4 * h + 4], x1_ss[:, 4 * h:4 * h + 4], ACT.Sqrt,
                                     bias=eps[:, :], scale=1.0 / H).then_inc(std2_set, 1)

            def std_x(s):
                act.wait_ge(route, route_at(s, "var4"))
                nc.scalar.activation(st_std[:, :], st_var4[:, :], ACT.Sqrt, bias=eps[:, :],
                                     scale=0.25).then_inc(std1_set, 1)

            def copy_xT(s, j):
                n = tile_no(s, j)
                act.wait_ge(x_T, n + 1)
                if j >= 2 or later(s):
                    act.wait_ge(scored, n - 1)
                nc.scalar.activation(xT[:, j % 2, :], ps_xT[:, :], ACT.Copy).then_inc(x_T_copied, 1)

            def square(g, j):
                n = tile_no(g, j)
                act.wait_ge(nmean_set, n + 1)
                if later(g):
                    act.wait_ge(std2_set, 2 * (g - 1) + j // 4 + 1)
                if j >= 1 or later(g):
                    act.wait_ge(squared, n)
                nc.scalar.activation(junk_a[:, :], x1[:, j, :], ACT.Square, bias=x1_nmean[:, j:j + 1],
                                     accum_out=x1_ss[:, j:j + 1]).then_inc(squared, 1)

            def high(g, j):
                n = tile_no(g, j)
                act.wait_ge(ln_T, n + 1)
                if j >= 2 or later(g):
                    act.wait_ge(multiplied, n - 1)
                nc.scalar.activation(hiT[:, j % 2, :], ps_lnT[:, :], ACT.Copy).then_inc(hi_set, 1)

            def make_base(g, j):
                n = tile_no(g, j)
                act.wait_ge(stats, half_at(STATS, g, j // 4, "base_bias"))
                if j >= 4 or later(g):
                    act.wait_ge(res_set, n - 3)
                nc.scalar.activation(base[:, j % 4, :], x1[:, j, :], ACT.Identity,
                                     bias=base_bias[:, j:j + 1], scale=base_scale[:, j:j + 1])\
                  .then_inc(base_set, 1)

            def normalise(g, j):
                n = tile_no(g, j)
                act.wait_ge(stats, half_at(STATS, g, j // 4, "base_bias"))
                if j >= 2 or later(g):
                    act.wait_ge(ln_T, n - 1)
                nc.scalar.activation(ln2[:, j % 2, :], x1[:, j, :], ACT.Identity,
                                     bias=ln_bias[:, j:j + 1], scale=ln_scale[:, j:j + 1])\
                  .then_inc(ln2_set, 1)

            def copy_ohT(g, h):
                act.wait_ge(oh_T, 2 * g + h + 1)
                if later(g):
                    act.wait_ge(enc_bcast, tile_no(g - 1, 4 * h + 4))
                nc.scalar.activation(ohT[:, 4 * h:4 * h + 4, :], ps_ohT[:, :, :], ACT.Copy)\
                  .then_inc(oh_T_copied, 1)

            def step(t):
                for i in range(TS):
                    if i == 0 and on(t - 4, NG):
                        std_x1(t - 4, 1)
                    if i == 4 and on(t - 3, NG):
                        std_x1(t - 3, 0)
                    if on(t - 4 + (i + 1) // TS, NG):
                        high(t - 4 + (i + 1) // TS, (i + 1) % TS)
                    if on(t, NS):
                        copy_xT(t, i)
                    if i == 1 and on(t - 3, NG):
                        copy_ohT(t - 3, 1)
                    if i == 7 and on(t - 2, NG):
                        copy_ohT(t - 2, 0)
                    if i == 2 and on(t - 1, NS):
                        std_x(t - 1)
                    if on(t - 4 + (i + 1) // TS, NG):
                        make_base(t - 4 + (i + 1) // TS, (i + 1) % TS)
                    if on(t - 4 + (i + 2) // TS, NG):
                        normalise(t - 4 + (i + 2) // TS, (i + 2) % TS)
                    if on(t - 3, NG):
                        square(t - 3, i)

            for t in range(5):
                step(t)
            with act.Fori(5, NS) as t:
                step(t)
            for t in range(NS, NG + 4):
                step(t)

        @block.tensor
        def _(pe):
            pe.wait_ge(const_in, 16)
            ident = table("ident")
            pe.wait_ge(gate_chain, 3)
            for c in range(HC):
                last = nc.tensor.transpose(ps_lnT[:, c * P:(c + 1) * P], g_rows[:, c * P:(c + 1) * P], ident)
            last.then_inc(gate_T, 1)
            for e in range(E):
                stage = (x_got, x1)[e % 2]
                pe.wait_ge(w_in[e % 2], 16 * (e // 2 + 1))
                for c in range(HC):
                    n = HC * e + c
                    if n >= 2:
                        pe.wait_ge(w_lo_set, n - 1)
                    for f in range(HC):
                        last = nc.tensor.transpose(ps_mm[:, c % 2, f * P:(f + 1) * P],
                                                   stage[:, f, c * P:(c + 1) * P], ident)
                    last.then_inc(w_T, 1)
            pe.wait_ge(gate_chain, 4)
            pe.wait_ge(tables_set, 1)

            def transpose_ln(g, j):
                n = tile_no(g, j)
                pe.wait_ge(ln2_set, n + 1)
                if j >= 1 or later(g):
                    pe.wait_ge(lo_set, n)
                for c in range(HC):
                    last = nc.tensor.transpose(ps_lnT[:, c * P:(c + 1) * P],
                                               ln2[:, j % 2, c * P:(c + 1) * P], ident)
                last.then_inc(ln_T, 1)

            def spread_enc(g, j):
                n = tile_no(g, j)
                if j % 4 == 0:
                    pe.wait_ge(oh_T_copied, 2 * g + j // 4 + 1)
                if j >= 1 or later(g):
                    pe.wait_ge(x1_set, n)
                if j in (0, 3):
                    rows = g + 1 + j // 3
                    pe.wait_ge(route, route_at(min(rows, NS - 1) if isinstance(g, int) else rows, "enc_table"))
                nc.tensor.matmul(ps_bcast[:, :], ohT[:, j, :], enc_tab[:, :], start=True, stop=True)\
                  .then_inc(enc_bcast, 1)

            def transpose_x(s, j):
                n = tile_no(s, j)
                if j % 4 == 0:
                    pe.wait_ge(x_loaded[j // 4], 16 * (s + 1))
                if j >= 1 or later(s):
                    pe.wait_ge(x_T_copied, n)
                for c in range(HC):
                    last = nc.tensor.transpose(ps_xT[:, c * P:(c + 1) * P],
                                               x_in[:, j, c * P:(c + 1) * P], ident)
                last.then_inc(x_T, 1)

            def score(s, j):
                n = tile_no(s, j)
                pe.wait_ge(x_T_copied, n + 1)
                if j == 0 and later(s):
                    pe.wait_ge(route, route_at(s - 1, "scores_copied"))
                for c in range(HC):
                    last = nc.tensor.matmul(ps_sc[:, j, :], xT[:, j % 2, c * P:(c + 1) * P], gates[:, c, :],
                                            start=(c == 0), stop=(c == HC - 1))
                last.then_inc(scored, 1)

            def score_enc(s):
                pe.wait_ge(route, route_at(s, "enc_rows1"))
                for b in range(2):
                    for c in range(HC):
                        last = nc.tensor.matmul(ps_es[:, b, :],
                                                enc_now[:, 4 * b + c:4 * b + c + 1].to_broadcast([P, P]),
                                                gates[:, c, 0:E], start=(c == 0), stop=(c == HC - 1))
                last.then_inc(enc_scored, 1)

            def enc_to_rows(s):
                if on(s - 2, NG):
                    pe.wait_ge(oh_T_copied, 2 * (s - 2) + 2)
                if later(s):
                    pe.wait_ge(route, route_at(s - 1, "enc_table"))
                for c in range(HC):
                    for b in range(2):
                        last = nc.tensor.matmul(ps_enc[:, c * P:(c + 1) * P],
                                                enc_lhs[:, 4 * b + c, :, :].rearrange("p k b -> p (k b)"),
                                                ident_b[:, :], start=(b == 0), stop=(b == 1))
                last.then_inc(enc_rowed, 1)

            def rank_tokens(s):
                pe.wait_ge(route, route_at(s, "onehot"))
                for k in range(TS + 1):
                    last = nc.tensor.matmul(ps_rank.rearrange("p t e -> p (t e)"),
                                            (ones_b if k else before_b)[:, :],
                                            onehot_pad[:, TS - k:2 * TS + 1 - k, :].rearrange("p t e -> p (t e)"),
                                            start=(k == 0), stop=(k == TS))
                last.then_inc(ranked, 1)

            def transpose_onehot(g, h):
                pe.wait_ge(oh_set, 2 * g + h + 1)
                if h or later(g):
                    pe.wait_ge(oh_T_copied, 2 * g + h)
                if h == 0 and on(g + 1, NS):
                    pe.wait_ge(route, route_at(g + 1, "enc_table"))
                for k in range(4):
                    last = nc.tensor.transpose(ps_ohT[:, k, :], oh[:, k, :], ident_b[:, :])
                last.then_inc(oh_T, 1)

            def multiply(g, j):
                n = tile_no(g, j)
                pe.wait_ge(hi_set, n + 1)
                pe.wait_ge(lo_set, n + 1)
                if j >= 2 or later(g):
                    pe.wait_ge(res_set, n - 1)
                if j == 0:
                    pe.wait_ge(pick, pick_at(g, "expert"))
                pe.wait_ge(tables_set, 1)
                e = pe.value_load(pick_expert[0:1, bass.ds(n, 1)], min_val=0, max_val=E - 1)
                k = 0
                for c in range(HC):
                    at = slice(c * H, (c + 1) * H)
                    xs = slice(c * P, (c + 1) * P)
                    for lhs, w in ((hiT, w_hi), (hiT, w_lo), (loT, w_hi)):
                        last = nc.tensor.matmul(ps_mm[:, j % 2, :], lhs[:, j % 2, xs],
                                                w[:, bass.ds(e, 1), at].rearrange("p a h -> p (a h)"),
                                                start=(k == 0), stop=(k == 3 * HC - 1))
                        k += 1
                last.then_inc(multiplied, 1)

            def step(t):
                for i in range(TS):
                    g, j = t - 4 + (i + 1) // TS, (i + 1) % TS
                    if on(g, NG):
                        transpose_ln(g, j)
                    if on(t - 3, NG):
                        spread_enc(t - 3, i)
                    if on(t, NS):
                        transpose_x(t, i)
                    if i == 1 and on(t - 3, NG):
                        transpose_onehot(t - 3, 1)
                    if i == 7 and on(t - 2, NG):
                        transpose_onehot(t - 2, 0)
                    if i == 1 and on(t - 1, NS):
                        score_enc(t - 1)
                    if i == 2 and on(t - 1, NS):
                        enc_to_rows(t - 1)
                    if i == 3 and on(t - 1, NS):
                        rank_tokens(t - 1)
                    if on(t - 4, NG):
                        multiply(t - 4, i)
                    if on(t, NS):
                        score(t, i)

            for t in range(5):
                step(t)
            with pe.Fori(5, NS) as t:
                step(t)
            for t in range(NS, NG + 4):
                step(t)

        @block.vector
        def _(dve):
            tt, ts, cp = nc.vector.tensor_tensor, nc.vector.tensor_scalar, nc.vector.tensor_copy
            stt, reduce = nc.vector.scalar_tensor_tensor, nc.vector.tensor_reduce

            nc.vector.memset(g_rows[:, :], 0.0).then_inc(rows_clear, 1)
            nc.vector.memset(eps[:, :], EPS)
            nc.vector.memset(ones_b[:, :], 1.0)
            nc.vector.memset(onehot_pad[:, :, :], 0.0)
            nc.vector.memset(enc_tab[:, :], 0.0)
            nc.vector.memset(done[:, :], 0.0)
            nc.vector.memset(ids_mix[:, :], 0)
            nc.vector.memset(enc_parts[:, :, 3:4], 0.0)
            dve.wait_ge(const_in, 16)
            cp(ident_b[:, :], table("ident"))
            cp(before_b[:, :], table("before"))
            cp(one31_b[:, :], table("one_at_31"))
            cp(counts[:, :], table("queue_start"))
            cp(next_ids[:, :], table("first_ids")).then_inc(tables_set, 1)
            dve.wait_ge(tables_set, 1)

            dve.wait_ge(gate_in, 32)
            reduce(g_sum[:, :], g_rows[:, :], AX.X, ALU.add).then_inc(gate_chain, 1)
            dve.wait_ge(gate_chain, 1)
            ts(g_sum[:, :], g_sum[:, :], -1.0 / H, None, ALU.mult).then_inc(gate_chain, 1)
            dve.wait_ge(gate_chain, 2)
            ts(g_rows[:, :], g_rows[:, :], g_sum[:, :], None, ALU.add).then_inc(gate_chain, 1)
            dve.wait_ge(gate_T, 1)
            cp(gates[:, :, :], ps_lnT[:, :].rearrange("p (c k) -> p c k", c=HC)[:, :, 0:E + 1])\
                .then_inc(gate_chain, 1)

            for e in range(E):
                stage = (x_got, x1)[e % 2]
                col = slice(e, e + 1)
                dve.wait_ge(w_in[e % 2], 16 * (e // 2 + 1))
                reduce(w_max[:, col], stage[:, 0:HC, :], AX.XY, ALU.max, apply_absolute_value=True)\
                    .then_inc(w_maxed, 1)
                dve.wait_ge(w_allmax, e + 1)
                ts(w_exp[:, col], w_amax[:, col].bitcast(I32), 23, None, ALU.logical_shift_right)\
                    .then_inc(w_chain, 1)
                dve.wait_ge(w_chain, 6 * e + 1)
                ts(w_exp[:, col], w_exp[:, col], W_TOP + LN_SHIFT + 1, None, ALU.max).then_inc(w_chain, 1)
                dve.wait_ge(w_chain, 6 * e + 2)
                ts(w_exp2[:, col], w_exp[:, col], -1.0, W_TOP + 254.0, ALU.mult, ALU.add).then_inc(w_chain, 1)
                ts(w_exp[:, col], w_exp[:, col], float(W_TOP + LN_SHIFT), None, ALU.subtract)\
                    .then_inc(w_chain, 1)
                dve.wait_ge(w_chain, 6 * e + 4)
                ts(w_scale[:, col], w_exp2[:, col], 23, None, ALU.logical_shift_left).then_inc(w_chain, 1)
                ts(w_unscale[:, col], w_exp[:, col], 23, None, ALU.logical_shift_left).then_inc(w_chain, 1)
                dve.wait_ge(w_chain, 6 * e + 6)
                for c in range(HC):
                    at = slice(c * H, (c + 1) * H)
                    dve.wait_ge(w_hi_set, HC * e + c + 1)
                    stt(w_lo[:, e, at], ps_mm[:, c % 2, :], w_scale[:, col].bitcast(FP32), w_hi[:, e, at],
                        ALU.mult, ALU.subtract).then_inc(w_lo_set, 1)
            dve.wait_ge(got_clear, 1)
            dve.wait_ge(small_in, 32)

            def routed(s, *names):
                dve.wait_ge(route, max(route_at(0, name) for name in names) + s * len(ROUTE))

            def route_slot0(s, gap):
                if gap == 0:
                    dve.wait_ge(scored, tile_no(s, TS))
                    cp(sc[:, :, :], ps_sc).then_inc(route, 1)
                    dve.wait_ge(ctx_dotted, tile_no(s, TS))
                    if later(s):
                        dve.wait_ge(enc_scored, s)
                    cp(enc_now[:, :], enc_col[:, :]).then_inc(route, 1)
                    dve.wait_ge(x_stats, tile_no(s, TS))
                    tt(st_diff[:, :], bn[:, :, 1], bn[:, :, 4], ALU.subtract).then_inc(route, 1)
                    tt(st_sum[:, :], bn[:, :, 2], bn[:, :, 5], ALU.add).then_inc(route, 1)
                if gap == 1:
                    if later(s):
                        dve.wait_ge(enc_rowed, s)
                    routed(s, "enc_copied")
                    cp(enc_parts[:, :, 0], enc_now[:, :]).then_inc(route, 1)
                if gap == 2:
                    routed(s, "enc_hi")
                    tt(enc_rest[:, :], enc_now[:, :], enc_parts[:, :, 0], ALU.subtract).then_inc(route, 1)
                if gap == 3:
                    routed(s, "enc_rest")
                    cp(enc_parts[:, :, 1], enc_rest[:, :]).then_inc(route, 1)
                if gap == 4:
                    routed(s, "enc_mid")
                    tt(enc_parts[:, :, 2], enc_rest[:, :], enc_parts[:, :, 1], ALU.subtract).then_inc(route, 1)
                if gap == 5:
                    routed(s, "enc_parts")
                    for b in range(2):
                        column = one31_b[:, bass.ds(31 - b - 2 * s, B)]
                        for j in range(4 * b, 4 * b + 4):
                            last = tt(enc_lhs[:, j, :, :],
                                      enc_parts[:, j, :].unsqueeze(2).to_broadcast([P, 4, B]),
                                      column.unsqueeze(1).to_broadcast([P, 4, B]), ALU.mult)
                        last.then_inc(route, 1)

            def route_slot1(s, gap):
                if gap == 0:
                    routed(s, "stat_diff")
                    tt(st_diff2[:, :], st_diff[:, :], st_diff[:, :], ALU.mult).then_inc(route, 1)
                if gap == 1:
                    routed(s, "stat_diff2")
                    stt(st_var4[:, :], st_sum[:, :], 4.0 / H, st_diff2[:, :], ALU.mult, ALU.add)\
                        .then_inc(route, 1)
                if gap == 3:
                    dve.wait_ge(enc_scored, s + 1)
                    tt(full_sc[:, :, :].rearrange("p (b j) e -> p b j e", b=2),
                       sc[:, :, 0:E].rearrange("p (b j) e -> p b j e", b=2),
                       ps_es.unsqueeze(2).to_broadcast([P, 2, 4, E]), ALU.add).then_inc(route, 1)
                if gap == 4:
                    routed(s, "scores")
                    reduce(best[:, :], full_sc[:, :, :], AX.X, ALU.max).then_inc(route, 1)
                if gap == 5:
                    routed(s, "best")
                    tt(is_best[:, :, :], full_sc[:, :, :], best[:, :].unsqueeze(2).to_broadcast([P, TS, E]),
                       ALU.is_ge).then_inc(route, 1)

            def route_slot2(s, gap):
                if gap == 0:
                    routed(s, "is_best")
                    tt(key[:, :, :], is_best[:, :, :],
                       table("first_key").unsqueeze(1).to_broadcast([P, TS, E]), ALU.mult).then_inc(route, 1)
                if gap == 1:
                    routed(s, "key")
                    reduce(best_key[:, :], key[:, :, :], AX.X, ALU.max).then_inc(route, 1)
                if gap == 2:
                    routed(s, "best_key")
                    if later(s):
                        dve.wait_ge(ranked, s)
                    tt(onehot, key[:, :, :], best_key[:, :].unsqueeze(2).to_broadcast([P, TS, E]),
                       ALU.is_equal).then_inc(route, 1)
                if gap == 3:
                    dve.wait_ge(std1_set, s + 1)
                    nc.vector.reciprocal(st_rstd[:, :], st_std[:, :]).then_inc(route, 1)
                if gap == 4:
                    routed(s, "rstd")
                    tt(st_d[:, :], sc[:, :, E], st_rstd[:, :], ALU.mult).then_inc(route, 1)
                if gap == 5:
                    dve.wait_ge(enc_rowed, s + 1)
                    if on(s - 2, NG) and later(s - 1):
                        dve.wait_ge(enc_bcast, tile_no(s - 2, 3))
                    tt(enc_tab[:, :], enc_tab[:, :], ps_enc[:, :], ALU.add).then_inc(route, 1)

            def route_slot3(s, gap):
                if gap == 0:
                    routed(s, "d_scaled")
                    if later(s):
                        dve.wait_ge(queued, 16 * TS * s)
                    ts(payload[:, :, 1].bitcast(FP32), st_d[:, :], bias[:, :], None, ALU.add).then_inc(route, 1)
                    cp(payload[:, :, 0], next_ids[:, :]).then_inc(route, 1)
                if gap == 1:
                    routed(s, "payload")
                    ts(next_ids[:, :], next_ids[:, :], float(STEP_TOKENS), None, ALU.add).then_inc(route, 1)
                    dve.wait_ge(ranked, s + 1)
                    tt(rank[:, :, :], ps_rank[:, 0:TS, :], counts[:, :].unsqueeze(1).to_broadcast([P, TS, E]),
                       ALU.add).then_inc(route, 1)
                if gap == 2:
                    routed(s, "rank")
                    tt(rank_own[:, :, :], rank[:, :, :], onehot, ALU.mult).then_inc(route, 1)
                    tt(counts[:, :], counts[:, :], ps_rank[:, TS, :], ALU.add).then_inc(route, 1)
                if gap == 3:
                    routed(s, "rank_own")
                    reduce(entry_f[:, :], rank_own[:, :, :], AX.X, ALU.add).then_inc(route, 1)
                if gap == 4:
                    routed(s, "entry_f")
                    cp(entry[:, :], entry_f[:, :]).then_inc(route, 1)

            def picked(g, name):
                dve.wait_ge(pick, pick_at(g, name))

            def spread(ap):
                return ap.unsqueeze(1).to_broadcast([P, TS, E])

            def pick_slot4(g, gap, all_routed):
                if gap == 0:
                    if not isinstance(g, int) or g + 1 < NS:
                        dve.wait_ge(route, route_at(g + 1, "counts"))
                    tt(full_i[:, :], counts[:, :], table("ceil_add" if all_routed else "floor_add"), ALU.add)\
                        .then_inc(pick, 1)
                    picked(g, "full_i")
                    ts(full[:, :], full_i[:, :], 7, None, ALU.logical_shift_right).then_inc(pick, 1)
                if gap == 1:
                    picked(g, "full")
                    tt(avail[:, :], full[:, :], done[:, :], ALU.subtract).then_inc(pick, 1)
                    picked(g, "avail")
                    tt(pre_t[:, :, :], avail[:, :].unsqueeze(1).to_broadcast([P, E, E]),
                       table("up_to").rearrange("p (a b) -> p a b", a=E), ALU.mult).then_inc(pick, 1)
                if gap == 2:
                    picked(g, "prefix_terms")
                    reduce(prefix[:, :], pre_t[:, :, :], AX.X, ALU.add).then_inc(pick, 1)
                if gap == 3:
                    picked(g, "prefix")
                    tt(passed[:, :, :], spread(prefix[:, :]),
                       table("pick").unsqueeze(2).to_broadcast([P, TS, E]), ALU.is_le).then_inc(pick, 1)
                    tt(start0[:, :], full[:, :], prefix[:, :], ALU.subtract).then_inc(pick, 1)
                if gap == 4:
                    picked(g, "start0")
                    reduce(expert_f[:, :], passed[:, :, :], AX.X, ALU.add).then_inc(pick, 1)
                    stt(start1[:, :], start0[:, :], float(P), table("queue_from_dummy"), ALU.mult, ALU.add)\
                        .then_inc(pick, 1)
                if gap == 5:
                    picked(g, "start1")
                    tt(chosen[:, :, :], spread(table("expert")),
                       expert_f[:, :].unsqueeze(2).to_broadcast([P, TS, E]), ALU.is_equal).then_inc(pick, 1)
                    picked(g, "chosen")
                    tt(start_t[:, :, :], chosen[:, :, :], spread(start1[:, :]), ALU.mult).then_inc(pick, 1)

            def pick_slot5(g, gap):
                here = bass.ds(tile_no(g, 0), TS)
                if gap == 0:
                    picked(g, "start_terms")
                    reduce(start_f[:, :], start_t[:, :, :], AX.X, ALU.add).then_inc(pick, 1)
                    picked(g, "start_f")
                    tt(pick_entry[:, here], start_f[:, :], table("pick_entry"), ALU.add).then_inc(pick, 1)
                if gap == 1:
                    ts(pick_expert[:, here], expert_f[:, :], float(E - 1), None, ALU.min).then_inc(pick, 1)
                    reduce(taken[:, :], chosen[:, :, :].rearrange("p i e -> p e i"), AX.X, ALU.add)\
                        .then_inc(pick, 1)
                if gap == 2:
                    picked(g, "taken")
                    tt(done[:, :], done[:, :], taken[:, :], ALU.add).then_inc(pick, 1)
                    tt(scale_t[:, :, :], chosen[:, :, :], spread(w_unscale[:, :].bitcast(FP32)), ALU.mult)\
                        .then_inc(pick, 1)
                if gap == 3:
                    picked(g, "scale_terms")
                    reduce(pick_scale[:, here], scale_t[:, :, :], AX.X, ALU.add).then_inc(pick, 1)

            def stats_done(g, h, name):
                dve.wait_ge(stats, half_at(STATS, g, h, name))

            def x1_stats(g, h):
                at = slice(4 * h, 4 * h + 4)
                dve.wait_ge(std2_set, 2 * g + h + 1)
                nc.vector.reciprocal(x1_rstd[:, at], x1_std[:, at]).then_inc(stats, 1)
                if later(g):
                    dve.wait_ge(base_set, tile_no(g - 1, 4 * h + 4))
                    dve.wait_ge(ln2_set, tile_no(g - 1, 4 * h + 4))
                stats_done(g, h, "rstd")
                ts(ln_scale[:, at], x1_rstd[:, at], float(1 << LN_SHIFT), None, ALU.mult).then_inc(stats, 1)
                stt(ln_bias[:, at], x1_nmean[:, at], float(1 << LN_SHIFT), x1_rstd[:, at], ALU.mult, ALU.mult)\
                    .then_inc(stats, 1)
                ts(base_scale[:, at], x1_rstd[:, at], 1.0, None, ALU.add).then_inc(stats, 1)
                tt(base_bias[:, at], x1_nmean[:, at], x1_rstd[:, at], ALU.mult).then_inc(stats, 1)

            def keep_ids(g, h):
                at = slice(4 * h, 4 * h + 4)
                if on(g - 2, NG):
                    for k in range(4):
                        dve.wait_ge(stored[k], 16 * (2 * (g - 2) + h + 1))
                if later(g):
                    dve.wait_ge(keep, half_at(KEEP, g - 1, h, "ids_mix"))
                cp(ids_out[:, at], ids_mix[:, at]).then_inc(keep, 1 if on(g, NG) else 2)
                if on(g, NG):
                    for k in range(4):
                        dve.wait_ge(meta_in[4 * h + k], 16 * (g + 1))
                    dve.wait_ge(keep, half_at(KEEP, g, h, "ids_out"))
                    cp(ids_mix[:, at], meta[:, at, 0].bitcast(U32)).then_inc(keep, 1)

            def onehot_batches(g, h):
                for k in range(4):
                    dve.wait_ge(meta_in[4 * h + k], 16 * (g + 1))
                at = slice(4 * h, 4 * h + 4)
                ts(batch_no[:, at], meta[:, at, 0], S.bit_length() - 1, None, ALU.logical_shift_right)\
                    .then_inc(batch_set, 1)
                dve.wait_ge(batch_set, 2 * g + h + 1)
                if h or later(g):
                    dve.wait_ge(oh_T, 2 * g + h)
                tt(oh[:, :, :], table("batch_of_col").unsqueeze(1).to_broadcast([P, 4, P]),
                   batch_no[:, at].unsqueeze(2).to_broadcast([P, 4, P]), ALU.is_equal).then_inc(oh_set, 1)

            def mix(g, j):
                n = tile_no(g, j)
                dve.wait_ge(enc_bcast, n + 1)
                dve.wait_ge(got[j], 16 * (g + 1))
                if later(g):
                    dve.wait_ge(base_set, tile_no(g - 1, j + 1))
                    dve.wait_ge(ln2_set, tile_no(g - 1, j + 1))
                    dve.wait_ge(squared, tile_no(g - 1, j + 1))
                stt(x1[:, j, :], x_got[:, j, :], meta[:, j, 1:2].bitcast(FP32), ps_bcast[:, :],
                    ALU.add, ALU.add, accum_out=x1_sum[:, j:j + 1]).then_inc(x1_set, 1)

            def negative_mean(g, j):
                dve.wait_ge(x1_set, tile_no(g, j) + 1)
                ts(x1_nmean[:, j:j + 1], x1_sum[:, j:j + 1], -1.0 / H, None, ALU.mult).then_inc(nmean_set, 1)

            def low(g, j):
                n = tile_no(g, j)
                dve.wait_ge(hi_set, n + 1)
                if j >= 2 or later(g):
                    dve.wait_ge(multiplied, n - 1)
                tt(loT[:, j % 2, :], ps_lnT[:, :], hiT[:, j % 2, :], ALU.subtract).then_inc(lo_set, 1)

            def finish(g, j):
                n = tile_no(g, j)
                dve.wait_ge(multiplied, n + 1)
                dve.wait_ge(base_set, n + 1)
                if j == 0:
                    dve.wait_ge(pick, pick_at(g, "scale"))
                if j >= 4 or later(g):
                    dve.wait_ge(stored[j % 4], 16 * (2 * g + j // 4))
                stt(res[:, j % 4, :], ps_mm[:, j % 2, :], pick_scale[:, bass.ds(n, 1)], base[:, j % 4, :],
                    ALU.mult, ALU.add).then_inc(res_set, 1)

            def dot_ctx(s, j):
                if j % 4 == 0:
                    dve.wait_ge(c_loaded[j // 4], 16 * (s + 1))
                if later(s):
                    dve.wait_ge(route, route_at(s - 1, "enc_copied"))
                stt(c_in[:, j, :], c_in[:, j, :], 1.0, w_enc[:, :], ALU.mult, ALU.mult,
                    accum_out=enc_col[:, j:j + 1]).then_inc(ctx_dotted, 1)

            def halves_stats(s, j):
                if j % 4 == 0:
                    dve.wait_ge(x_loaded[j // 4], 16 * (s + 1))
                nc.vector.bn_stats(bn[:, j, :], x_in[:, j, :]).then_inc(x_stats, 1)

            def step(t):
                def between(i, gap):
                    if gap == 0 and i == 0 and on(t - 4, NG):
                        x1_stats(t - 4, 1)
                    if gap == 0 and i == 5 and on(t - 3, NG):
                        x1_stats(t - 3, 0)
                    if on(t - 1, NS):
                        if i < 4:
                            (route_slot0, route_slot1, route_slot2, route_slot3)[i](t - 1, gap)
                    if on(t - 2, NG):
                        if i == 4:
                            pick_slot4(t - 2, gap, isinstance(t, int) and t >= NS)
                        if i == 5:
                            pick_slot5(t - 2, gap)

                for i in range(TS):
                    if i in (0, 4) and on(t - 3, NG + 1):
                        keep_ids(t - 3, i // 4)
                    if i == 1 and on(t - 3, NG):
                        onehot_batches(t - 3, 1)
                    if i == 7 and on(t - 2, NG):
                        onehot_batches(t - 2, 0)
                    between(i, 0)
                    if on(t - 4 + (i - 1) // TS, NG):
                        finish(t - 4 + (i - 1) // TS, (i - 1) % TS)
                    between(i, 1)
                    if on(t - 3, NG):
                        mix(t - 3, i)
                    between(i, 2)
                    if on(t, NS):
                        dot_ctx(t, i)
                    between(i, 3)
                    if on(t - 3, NG):
                        negative_mean(t - 3, i)
                    if on(t - 4 + (i + 1) // TS, NG):
                        low(t - 4 + (i + 1) // TS, (i + 1) % TS)
                    between(i, 4)
                    if on(t, NS):
                        halves_stats(t, i)
                    between(i, 5)

            for t in range(5):
                step(t)
            with dve.Fori(5, NS) as t:
                step(t)
            for t in range(NS, NG + 4):
                step(t)
            finish(NG - 1, TS - 1)


_INS = ['x', 'ctx_1024', 'L0_xattn_mlp_weight', 'L0_xattn_mlp_bias', 'L0_ffn_gate_w', 'L0_ffn_expert_w']


def kernel(**inputs):
    import numpy as _np
    import concourse.bacc as _bacc
    from concourse import mybir as _mybir
    from concourse.bass_utils import run_bass_kernel_spmd as _run

    nc = _bacc.Bacc("TRN2", target_bir_lowering=False, num_devices=1)
    const, cols = constants()
    arrays, args = {}, []
    for name, a in [(n, inputs[n]) for n in _INS] + [("const", const)]:
        a = _np.ascontiguousarray(a)
        arrays[f"in_{name}"] = a
        args.append(nc.dram_tensor(f"in_{name}", a.shape, _mybir.dt.from_np(a.dtype), kind="ExternalInput").ap())
    out = nc.dram_tensor("out_0", (B, S, H), _mybir.dt.float32, kind="ExternalOutput").ap()
    build(nc, *args, cols, out)
    r = _run(nc, [arrays], core_ids=[0])
    return r.results[0]["out_0"]
```

```python
import concourse.bass as bass
from concourse import mybir
from contextlib import ExitStack
import numpy as np

FP32 = mybir.dt.float32
FP16 = mybir.dt.float16
BF16 = mybir.dt.bfloat16
I32 = mybir.dt.int32
U32 = mybir.dt.uint32
ALU = mybir.AluOpType
ACT = mybir.ActivationFunctionType
AX = mybir.AxisListType

P = 128
B, S, H, E = 32, 512, 512, 8
N = B * S
HC = H // P
TS = 8
STEP_TOKENS = TS * P
NS = N // STEP_TOKENS
NG = (N + E * (P - 1)) // P // TS + 1
QUEUE = N + P
DUMMY = E * QUEUE
ENTRIES = DUMMY + TS * P
NO_TOKEN = 1 << 20
EPS = 1e-5
SHIFT_OF = 32
W_TOP = 13
LN_SHIFT = 8
assert ENTRIES % P == 0



def constants():
    p = np.arange(P)[:, None]
    e = np.arange(E)
    j = np.arange(TS)
    c = np.arange(P)
    parts = {
        "ident": (c[None] == p),
        "before": (p < c[None]),
        "batch_of_col": np.where(c < 3 * B, c % B, -1)[None],
        "one_at_31": (np.arange(64) == 31)[None],
        "up_to": np.tril(np.ones((E, E))).reshape(1, -1),
        "first_key": (E - e)[None],
        "expert": e[None],
        "pick": j[None],
        "queue_start": (e * QUEUE)[None],
        "floor_add": (-e * QUEUE)[None],
        "ceil_add": (P - 1 - e * QUEUE)[None],
        "queue_from_dummy": (e * QUEUE - DUMMY)[None],
        "pick_entry": (j * P + DUMMY)[None],
        "first_ids": j[None] * P + p,
    }
    at, cols, out = 0, {}, []
    for name, a in parts.items():
        a = np.broadcast_to(np.asarray(a, np.float32), (P, np.asarray(a).shape[1]))
        cols[name] = (at, at + a.shape[1])
        at += a.shape[1]
        out.append(a)
    return np.ascontiguousarray(np.concatenate(out, 1)), cols


ROUTE = ["scores_copied", "enc_copied", "diff", "diff2", "var", "scores", "best", "is_best",
         "key", "best_key", "onehot", "rstd", "d_scaled", "payload_d", "payload", "next_ids",
         "rank", "rank_own", "counts", "entry_f", "enc_table", "entry"]
ENC = ["hi", "rest", "mid", "parts", "columns"]
PICK = ["full_i", "full", "avail", "prefix_terms", "prefix", "passed", "start0", "expert_f", "start1",
        "chosen", "start_terms", "start_f", "entry", "expert", "taken", "done"]
SCALE = ["is_expert", "scale_terms", "scale"]
STATS = ["rstd", "ln_scale", "ln_bias", "base_scale", "base_bias"]
KEEP = ["ids_out", "ids_mix"]


def build(nc, x, ctx, mlp_weight, mlp_bias, gate_w, expert_w, const, cols, out):
    x_rows = x.rearrange("b s h -> (b s) h")
    out_rows = out.rearrange("b s h -> (b s) h")
    queue = nc.dram_tensor("queue", [ENTRIES, 2], I32, kind="Internal").ap()

    with ExitStack() as stack:
        def sb(name, shape, dt):
            return stack.enter_context(nc.sbuf_tensor(name, shape, dt))

        def pb(name, shape, dt):
            return stack.enter_context(nc.psum_tensor(name, shape, dt))

        def sem(name):
            return stack.enter_context(nc.semaphore(name))

        cst = sb("cst", [P, const.shape[1]], FP32)

        def table(name):
            return cst[:, cols[name][0]:cols[name][1]]
        ident_b = sb("ident_b", [P, P], BF16)
        before_b = sb("before_b", [P, P], BF16)
        ones_b = sb("ones_b", [P, P], BF16)
        batch_of_col_b = sb("batch_of_col_b", [P, P], BF16)
        one31_b = sb("one31_b", [P, 64], BF16)
        w_hi = sb("w_hi", [P, E, HC * H], FP16)
        w_lo = sb("w_lo", [P, E, HC * H], FP16)
        w_enc = sb("w_enc", [P, H], FP32)
        bias = sb("bias", [P, 1], FP32)
        eps = sb("eps", [P, 1], FP32)
        g_rows = sb("g_rows", [P, H], FP32)
        g_sum = sb("g_sum", [P, 1], FP32)
        gates = sb("gates", [P, HC, E + 2], FP32)
        w_max = sb("w_max", [P, E], FP32)
        w_amax = sb("w_amax", [P, E], FP32)
        w_exp = sb("w_exp", [P, E], I32)
        w_exp2 = sb("w_exp2", [P, E], I32)
        w_scale = sb("w_scale", [P, E], I32)
        w_unscale = sb("w_unscale", [P, E], I32)
        x_in = sb("x_in", [P, TS, H], FP32)
        c_in = sb("c_in", [P, TS, H], FP32)
        xT = sb("xT", [P, 2, HC * P], FP32)
        junk_x = sb("junk_x", [P, H], FP32)
        junk_x1 = sb("junk_x1", [P, H], FP32)
        enc_col = sb("enc_col", [P, TS], FP32)
        x_shift = sb("x_shift", [P, TS], FP32)
        x_ss = sb("x_ss", [P, TS], FP32)
        sc = sb("sc", [P, TS, E + 2], FP32)
        enc_now = sb("enc_now", [P, TS], FP32)
        enc_parts = sb("enc_parts", [P, TS, 4], BF16)
        enc_rest = sb("enc_rest", [P, TS], FP32)
        enc_lhs = sb("enc_lhs", [P, TS, 4, B], BF16)
        enc_tab = sb("enc_tab", [P, H], BF16)
        st_diff = sb("st_diff", [P, TS], FP32)
        st_diff2 = sb("st_diff2", [P, TS], FP32)
        st_var = sb("st_var", [P, TS], FP32)
        st_std = sb("st_std", [P, TS], FP32)
        st_rstd = sb("st_rstd", [P, TS], FP32)
        st_d = sb("st_d", [P, TS], FP32)
        full_sc = sb("full_sc", [P, TS, E], FP32)
        best = sb("best", [P, TS], FP32)
        is_best = sb("is_best", [P, TS, E], FP32)
        key = sb("key", [P, TS, E], FP32)
        best_key = sb("best_key", [P, TS], FP32)
        onehot_pad = sb("onehot_pad", [P, 2 * TS + 1, E], BF16)
        onehot = onehot_pad[:, TS:2 * TS, :]
        counts = sb("counts", [P, E], FP32)
        rank = sb("rank", [P, TS, E], FP32)
        rank_own = sb("rank_own", [P, TS, E], FP32)
        entry_f = sb("entry_f", [P, TS], FP32)
        entry = sb("entry", [P, TS], U32)
        next_ids = sb("next_ids", [P, TS], FP32)
        payload = sb("payload", [P, TS, 2], I32)
        full_i = sb("full_i", [P, E], I32)
        full = sb("full", [P, E], I32)
        avail = sb("avail", [P, E], FP32)
        done = sb("done", [P, E], FP32)
        pre_t = sb("pre_t", [P, E, E], FP32)
        prefix = sb("prefix", [P, E], FP32)
        passed = sb("passed", [P, TS, E], FP32)
        expert_f = sb("expert_f", [P, TS], FP32)
        chosen = sb("chosen", [P, TS, E], FP32)
        start0 = sb("start0", [P, E], FP32)
        start1 = sb("start1", [P, E], FP32)
        start_t = sb("start_t", [P, TS, E], FP32)
        start_f = sb("start_f", [P, TS], FP32)
        taken = sb("taken", [P, E], FP32)
        is_expert = sb("is_expert", [P, TS, E], FP32)
        scale_t = sb("scale_t", [P, TS, E], FP32)
        pick_entry = sb("pick_entry", [P, NG * TS], I32)
        pick_expert = sb("pick_expert", [P, NG * TS], I32)
        pick_scale = sb("pick_scale", [P, NG * TS], FP32)
        meta = sb("meta", [P, TS, 2], I32)
        batch_no = sb("batch_no", [P, TS], I32)
        oh = sb("oh", [P, TS // 2, P], BF16)
        ohT = sb("ohT", [P, TS, P], BF16)
        x_got = sb("x_got", [P, TS, H], FP32)
        x1 = sb("x1", [P, TS, H], FP32)
        x1_sum = sb("x1_sum", [P, TS], FP32)
        x1_nmean = sb("x1_nmean", [P, TS], FP32)
        x1_ss = sb("x1_ss", [P, TS], FP32)
        x1_std = sb("x1_std", [P, TS], FP32)
        x1_rstd = sb("x1_rstd", [P, TS], FP32)
        ln_scale = sb("ln_scale", [P, TS], FP32)
        ln_bias = sb("ln_bias", [P, TS], FP32)
        base_scale = sb("base_scale", [P, TS], FP32)
        base_bias = sb("base_bias", [P, TS], FP32)
        ids_mix = sb("ids_mix", [P, TS], U32)
        ids_out = sb("ids_out", [P, TS], U32)
        ln2 = sb("ln2", [P, 2, H], FP32)
        hiT = sb("hiT", [P, 2, HC * P], FP16)
        loT = sb("loT", [P, 2, HC * P], FP16)
        base = sb("base", [P, 4, H], FP32)
        res = sb("res", [P, 4, H], FP32)

        w_stage = (base, res)

        ps_xT = pb("ps_xT", [P, HC * P], FP32)
        ps_scores = pb("ps_scores", [P, 512], FP32)
        ps_rows = pb("ps_rows", [P, 512], FP32)
        ps_route = pb("ps_route", [P, 512], FP32)
        ps_bcast = pb("ps_bcast", [P, H], FP32)
        ps_lnT = pb("ps_lnT", [P, HC * P], FP32)
        ps_mm = pb("ps_mm", [P, 2, H], FP32)
        ps_sc = ps_scores[:, 0:TS * (E + 2)].rearrange("p (t e) -> p t e", e=E + 2)
        ps_enc = ps_rows[:, 0:H]
        ps_ohT = ps_rows[:, 0:4 * P // 2].bitcast(BF16).rearrange("p (t c) -> p t c", c=P)
        ps_es = ps_route[:, 0:2 * E].rearrange("p (b e) -> p b e", e=E)
        ps_rank = ps_route[:, 128:128 + (TS + 1) * E].rearrange("p (t e) -> p t e", e=E)

        const_in = sem("const_in")
        small_in = sem("small_in")
        gate_in = sem("gate_in")
        queue_fill = sem("queue_fill")
        queue_filled = sem("queue_filled")
        tables_set = sem("tables_set")
        rows_clear = sem("rows_clear")
        gate_chain = sem("gate_chain")
        gate_T = sem("gate_T")
        w_in = [sem(f"w_in{k}") for k in range(2)]
        w_maxed = sem("w_maxed")
        w_allmax = sem("w_allmax")
        w_chain = sem("w_chain")
        w_T = sem("w_T")
        w_hi_set = sem("w_hi_set")
        w_lo_set = sem("w_lo_set")
        got_clear = sem("got_clear")
        x_loaded = [sem(f"x_loaded{k}") for k in range(2)]
        c_loaded = [sem(f"c_loaded{k}") for k in range(2)]
        x_T = sem("x_T")
        x_T_copied = sem("x_T_copied")
        scored = sem("scored")
        ctx_dotted = sem("ctx_dotted")
        x_shifted = sem("x_shifted")
        x_squared = sem("x_squared")
        route = sem("route")
        enc_split = sem("enc_split")
        enc_scored = sem("enc_scored")
        enc_rowed = sem("enc_rowed")
        ranked = sem("ranked")
        std1_set = sem("std1_set")
        queued = sem("queued")
        pool_waited = sem("pool_waited")
        sp_waited = sem("sp_waited")
        pick = sem("pick")
        scale = sem("scale")
        meta_in = [sem(f"meta_in{j}") for j in range(TS)]
        got = [sem(f"got{j}") for j in range(TS)]
        keep = sem("keep")
        batch_set = sem("batch_set")
        oh_set = sem("oh_set")
        oh_T = sem("oh_T")
        oh_T_copied = sem("oh_T_copied")
        enc_bcast = sem("enc_bcast")
        x1_set = sem("x1_set")
        nmean_set = sem("nmean_set")
        squared = sem("squared")
        std2_set = sem("std2_set")
        stats = sem("stats")
        ln2_set = sem("ln2_set")
        ln_T = sem("ln_T")
        hi_set = sem("hi_set")
        lo_set = sem("lo_set")
        base_set = sem("base_set")
        multiplied = sem("multiplied")
        res_set = sem("res_set")
        stored = [sem(f"stored{k}") for k in range(4)]

        def route_at(s, name):
            return s * len(ROUTE) + (ROUTE.index(name) + 1)

        def pick_at(g, name):
            return g * len(PICK) + (PICK.index(name) + 1)

        def scale_at(g, name):
            return g * len(SCALE) + (SCALE.index(name) + 1)

        def half_at(chain, g, h, name):
            return (2 * g + h) * len(chain) + (chain.index(name) + 1)

        def tile_no(g, j):
            return g * TS + j

        def mixed(t, i):
            return t - 3 + (i - 2) // TS, (i - 2) % TS

        def ahead(t, i, k):
            return t - 4 + (i + k) // TS, (i + k) % TS

        def x_ahead(t, i):
            return t + (i + 1) // TS, (i + 1) % TS

        def prepared(t, i):
            if isinstance(t, int) and t < E // 2 and i >= 4:
                return [(2 * t + (i - 4) // 2, 2 * (i % 2) + k) for k in range(2)]
            return []

        def on(k, count):
            return not isinstance(k, int) or 0 <= k < count

        def later(k):
            return not isinstance(k, int) or k > 0

        block = stack.enter_context(nc.Block())

        @block.sync
        def _(sp):
            sp.dma_start(cst[:, :], const).then_inc(const_in, 16)
            sp.wait_ge(rows_clear, 1)
            sp.dma_start(g_rows[0:E, :], gate_w).then_inc(gate_in, 16)
            sp.dma_start(g_rows[E:E + 1, :], mlp_weight[:, H:2 * H]).then_inc(gate_in, 16)
            sp.dma_start(w_enc[:, :], mlp_weight[:, 0:H].partition_broadcast(P)).then_inc(small_in, 16)
            sp.dma_start(bias[:, :], mlp_bias.partition_broadcast(P)).then_inc(small_in, 16)
            sp.wait_ge(queue_fill, 1)
            sp.dma_start(queue.rearrange("(p n) c -> p (n c)", p=P),
                         x1[:, :, :].rearrange("p t h -> p (t h)").bitcast(I32)[:, 0:2 * ENTRIES // P])\
              .then_inc(queue_filled, 16)

            def alone(semaphore, value):
                sp.wait_ge(semaphore, value)
                sp.sem_inc(sp_waited, 1)

            def load_half(s, h):
                if later(s):
                    alone(x_T, tile_no(s - 1, 4 * h + 4))
                    alone(x_squared, tile_no(s - 1, 4 * h + 4))
                    alone(ctx_dotted, tile_no(s - 1, 4 * h + 4))
                src = 2 * s + h
                for dst, dram, arrived in ((x_in, x, x_loaded[h]), (c_in, ctx, c_loaded[h])):
                    sp.dma_start(dst[:, 4 * h:4 * h + 4, :],
                                 dram[bass.ds(src, 1), :, :].rearrange("a (j p) h -> p (a j) h", p=P))\
                      .then_inc(arrived, 16)

            def load_weights(e):
                if e >= 2:
                    alone(w_lo_set, HC * (e - 1))
                sp.dma_start(w_stage[e % 2][:, :, :], expert_w[e].rearrange("(c p) h -> p c h", p=P))\
                  .then_inc(w_in[e % 2], 16)

            def read_meta(g, j):
                if later(g):
                    alone(x1_set, tile_no(g - 1, j + 1))
                    alone(keep, half_at(KEEP, g - 1, j // 4, "ids_mix"))
                    alone(batch_set, 2 * (g - 1) + j // 4 + 1)
                    alone(got[j], 16 * g)
                at = sp.value_load(pick_entry[0:1, bass.ds(tile_no(g, j), 1)], min_val=0, max_val=ENTRIES - P)
                sp.dma_start(meta[:, j, :], queue[bass.ds(at, P), :]).then_inc(meta_in[j], 16)

            for h in range(2):
                load_half(0, h)
                load_weights(h)

            def step(t):
                s, g = t, t - 2
                if on(s + 1, NS):
                    load_half(s + 1, 0)
                if isinstance(t, int) and 2 * t + 2 < E:
                    load_weights(2 * t + 2)
                if on(g, NG):
                    alone(pick, pick_at(g, "entry"))
                    routed = g + 1 if not isinstance(g, int) else min(g + 1, NS - 1)
                    alone(queued, 16 * TS * (routed + 1))
                    for j in range(6):
                        read_meta(g, j)
                if on(s + 1, NS):
                    load_half(s + 1, 1)
                if isinstance(t, int) and 2 * t + 3 < E:
                    load_weights(2 * t + 3)
                if on(g, NG):
                    for j in range(6, TS):
                        read_meta(g, j)

            for t in range(5):
                step(t)
            with sp.Fori(5, NS - 1) as t:
                step(t)
            for t in range(NS - 1, NG + 4):
                step(t)
            for k in range(4):
                sp.wait_ge(stored[k], 16 * (NG * TS // 4))

        @block.gpsimd
        def _(pool):
            nc.gpsimd.memset(x1[:, :, :].rearrange("p t h -> p (t h)").bitcast(I32)[:, 0:2 * ENTRIES // P],
                             NO_TOKEN).then_inc(queue_fill, 1)
            nc.gpsimd.memset(x_got[:, :, :], 0.0).then_inc(got_clear, 1)
            pool.wait_ge(got_clear, 1)
            pool.wait_ge(tables_set, 1)

            def widest(e):
                pool.wait_ge(w_maxed, e + 1)
                nc.gpsimd.partition_all_reduce(w_amax[:, e:e + 1], w_max[:, e:e + 1], P,
                                               bass.bass_isa.ReduceOp.absmax).then_inc(w_allmax, 1)

            def plain(value, semaphore):
                pool.wait_ge(semaphore, value)
                pool.sem_inc(pool_waited, 1)

            def enqueue(s, j):
                if isinstance(s, int) and s == 0 and j == 0:
                    pool.wait_ge(queue_filled, 16)
                plain(route_at(s, "entry"), route)
                pool.indirect_dma_start(queue, bass.IndirectOffsetOnAxis(ap=entry[:, j:j + 1], axis=0),
                                        payload[:, j, :], None,
                                        bounds_check=ENTRIES - 1, oob_is_err=False).then_inc(queued, 16)

            def gather(g, j):
                if later(g):
                    plain(tile_no(g - 1, j + 1), x1_set)
                plain(16 * (g + 1), meta_in[j])
                pool.indirect_dma_start(x_got[:, j, :], None, x_rows,
                                        bass.IndirectOffsetOnAxis(ap=meta[:, j, 0:1].bitcast(U32), axis=0),
                                        bounds_check=N - 1, oob_is_err=False).then_inc(got[j], 16)

            def scatter(g, j):
                plain(half_at(KEEP, g + 1, j // 4, "ids_out"), keep)
                plain(tile_no(g, j + 1), res_set)
                pool.indirect_dma_start(out_rows, bass.IndirectOffsetOnAxis(ap=ids_out[:, j:j + 1], axis=0),
                                        res[:, j % 4, :], None,
                                        bounds_check=N - 1, oob_is_err=False).then_inc(stored[j % 4], 16)

            def enc_at(s, name):
                return s * len(ENC) + (ENC.index(name) + 1)

            def split_enc(s):
                tt, cp = nc.gpsimd.tensor_tensor, nc.gpsimd.tensor_copy
                if later(s):
                    plain(s, enc_rowed)
                plain(route_at(s, "enc_copied"), route)
                cp(enc_parts[:, :, 0], enc_now[:, :]).then_inc(enc_split, 1)
                plain(enc_at(s, "hi"), enc_split)
                tt(enc_rest[:, :], enc_now[:, :], enc_parts[:, :, 0], ALU.subtract).then_inc(enc_split, 1)
                plain(enc_at(s, "rest"), enc_split)
                cp(enc_parts[:, :, 1], enc_rest[:, :]).then_inc(enc_split, 1)
                plain(enc_at(s, "mid"), enc_split)
                tt(enc_parts[:, :, 2], enc_rest[:, :], enc_parts[:, :, 1], ALU.subtract).then_inc(enc_split, 1)
                plain(enc_at(s, "parts"), enc_split)
                for b in range(2):
                    column = one31_b[:, bass.ds(31 - b - 2 * s, B)]
                    for j in range(4 * b, 4 * b + 4):
                        last = tt(enc_lhs[:, j, :, :], enc_parts[:, j, :].unsqueeze(2).to_broadcast([P, 4, B]),
                                  column.unsqueeze(1).to_broadcast([P, 4, B]), ALU.mult)
                last.then_inc(enc_split, 1)

            gathers = {7: (0, 1, 2), 8: (3, 4), 9: (5,), 10: (6,), 11: (7,)}

            def step(t):
                for i in range(TS):
                    for j in gathers.get(i + TS, ()):
                        if on(t - 3, NG):
                            gather(t - 3, j)
                    if on(ahead(t, i, -1)[0], NG):
                        scatter(*ahead(t, i, -1))
                    if i == 0 and on(t - 1, NS):
                        split_enc(t - 1)
                    if isinstance(t, int) and t < E // 2 and i in (2, 4):
                        widest(2 * t + (i - 2) // 2)
                    if i in (4, 5) and on(t - 1, NS):
                        for j in range(4 * (i - 4), 4 * (i - 4) + 4):
                            enqueue(t - 1, j)
                    for j in gathers.get(i, ()):
                        if on(t - 2, NG):
                            gather(t - 2, j)

            for t in range(5):
                step(t)
            with pool.Fori(5, NS) as t:
                step(t)
            for t in range(NS, NG + 4):
                step(t)
            scatter(NG - 1, 7)

        @block.scalar
        def _(act):
            act.wait_ge(tables_set, 1)

            def split_high(e, c):
                act.wait_ge(w_T, HC * e + c + 1)
                act.wait_ge(w_chain, 6 * (e + 1))
                nc.scalar.activation(w_hi[:, e, c * H:(c + 1) * H], ps_mm[:, c % 2, :], ACT.Copy,
                                     scale=w_scale[:, e:e + 1].bitcast(FP32)).then_inc(w_hi_set, 1)

            def std_x1(g, h):
                act.wait_ge(squared, tile_no(g, 4 * h + 4))
                if later(g):
                    act.wait_ge(stats, half_at(STATS, g - 1, h, "rstd"))
                nc.scalar.activation(x1_std[:, 4 * h:4 * h + 4], x1_ss[:, 4 * h:4 * h + 4], ACT.Sqrt,
                                     bias=eps[:, :], scale=1.0 / H).then_inc(std2_set, 1)

            def std_x(s):
                act.wait_ge(route, route_at(s, "var"))
                nc.scalar.activation(st_std[:, :], st_var[:, :], ACT.Sqrt, bias=eps[:, :]).then_inc(std1_set, 1)

            def copy_xT(s, j):
                n = tile_no(s, j)
                act.wait_ge(x_T, n + 1)
                if j >= 2 or later(s):
                    act.wait_ge(scored, n - 1)
                nc.scalar.activation(xT[:, j % 2, :], ps_xT[:, :], ACT.Copy).then_inc(x_T_copied, 1)

            def square_x(s, j):
                act.wait_ge(x_shifted, 2 * s + j // 4 + 1)
                if later(s) and j == 0:
                    act.wait_ge(route, route_at(s - 1, "var"))
                if later(s) or j > 0:
                    act.wait_ge(x_squared, tile_no(s, j))
                nc.scalar.activation(junk_x[:, :], x_in[:, j, :], ACT.Square, bias=x_shift[:, j:j + 1],
                                     scale=-float(SHIFT_OF), accum_out=x_ss[:, j:j + 1]).then_inc(x_squared, 1)

            def square(g, j):
                n = tile_no(g, j)
                act.wait_ge(nmean_set, n + 1)
                if later(g):
                    act.wait_ge(std2_set, 2 * (g - 1) + j // 4 + 1)
                if j >= 1 or later(g):
                    act.wait_ge(squared, n)
                nc.scalar.activation(junk_x1[:, :], x1[:, j, :], ACT.Square, bias=x1_nmean[:, j:j + 1],
                                     accum_out=x1_ss[:, j:j + 1]).then_inc(squared, 1)

            def high(g, j):
                n = tile_no(g, j)
                act.wait_ge(ln_T, n + 1)
                if j >= 2 or later(g):
                    act.wait_ge(multiplied, n - 1)
                nc.scalar.activation(hiT[:, j % 2, :], ps_lnT[:, :], ACT.Copy).then_inc(hi_set, 1)

            def make_base(g, j):
                n = tile_no(g, j)
                act.wait_ge(stats, half_at(STATS, g, j // 4, "base_bias"))
                if j >= 4 or later(g):
                    act.wait_ge(res_set, n - 3)
                nc.scalar.activation(base[:, j % 4, :], x1[:, j, :], ACT.Identity,
                                     bias=base_bias[:, j:j + 1], scale=base_scale[:, j:j + 1])\
                  .then_inc(base_set, 1)

            def normalise(g, j):
                n = tile_no(g, j)
                act.wait_ge(stats, half_at(STATS, g, j // 4, "base_bias"))
                if j >= 2 or later(g):
                    act.wait_ge(ln_T, n - 1)
                nc.scalar.activation(ln2[:, j % 2, :], x1[:, j, :], ACT.Identity,
                                     bias=ln_bias[:, j:j + 1], scale=ln_scale[:, j:j + 1])\
                  .then_inc(ln2_set, 1)

            def copy_ohT(g, h):
                act.wait_ge(oh_T, 2 * g + h + 1)
                if later(g):
                    act.wait_ge(enc_bcast, tile_no(g - 1, 4 * h + 4))
                nc.scalar.activation(ohT[:, 4 * h:4 * h + 4, :], ps_ohT[:, :, :], ACT.Copy)\
                  .then_inc(oh_T_copied, 1)

            def step(t):
                for i in range(TS):
                    if i == 2 and on(t - 4, NG):
                        std_x1(t - 4, 1)
                    if i == 6 and on(t - 3, NG):
                        std_x1(t - 3, 0)
                    if on(ahead(t, i, 1)[0], NG):
                        high(*ahead(t, i, 1))
                    if on(x_ahead(t, i)[0], NS):
                        copy_xT(*x_ahead(t, i))
                    if i in (1, 4) and on(t - 3, NG):
                        copy_ohT(t - 3, i // 4)
                    if i == 2 and on(t - 1, NS):
                        std_x(t - 1)
                    if on(ahead(t, i, 1)[0], NG):
                        make_base(*ahead(t, i, 1))
                    if on(ahead(t, i, 2)[0], NG):
                        normalise(*ahead(t, i, 2))
                    if on(mixed(t, i)[0], NG):
                        square(*mixed(t, i))
                    if on(t, NS):
                        square_x(t, i)
                    for e, c in prepared(t, i):
                        split_high(e, c)

            copy_xT(0, 0)
            for t in range(5):
                step(t)
            with act.Fori(5, NS - 1) as t:
                step(t)
            for t in range(NS - 1, NG + 4):
                step(t)

        @block.tensor
        def _(pe):
            pe.wait_ge(const_in, 16)
            ident = table("ident")
            pe.wait_ge(gate_chain, 3)
            for c in range(HC):
                last = nc.tensor.transpose(ps_lnT[:, c * P:(c + 1) * P], g_rows[:, c * P:(c + 1) * P], ident)
            last.then_inc(gate_T, 1)
            pe.wait_ge(gate_chain, 4)

            def transpose_weights(e, c):
                n = HC * e + c
                pe.wait_ge(w_in[e % 2], 16 * (e // 2 + 1))
                if n >= 2:
                    pe.wait_ge(w_lo_set, n - 1)
                for f in range(HC):
                    last = nc.tensor.transpose(ps_mm[:, c % 2, f * P:(f + 1) * P],
                                               w_stage[e % 2][:, f, c * P:(c + 1) * P], ident)
                last.then_inc(w_T, 1)

            def transpose_ln(g, j):
                n = tile_no(g, j)
                pe.wait_ge(ln2_set, n + 1)
                if j >= 1 or later(g):
                    pe.wait_ge(lo_set, n)
                for c in range(HC):
                    last = nc.tensor.transpose(ps_lnT[:, c * P:(c + 1) * P],
                                               ln2[:, j % 2, c * P:(c + 1) * P], ident)
                last.then_inc(ln_T, 1)

            def spread_enc(g, j):
                n = tile_no(g, j)
                if j % 4 == 0:
                    pe.wait_ge(oh_T_copied, 2 * g + j // 4 + 1)
                if j >= 1 or later(g):
                    pe.wait_ge(x1_set, n)
                if j in (0, 2):
                    rows = g + 1 + j // 2
                    pe.wait_ge(route, route_at(min(rows, NS - 1) if isinstance(g, int) else rows, "enc_table"))
                nc.tensor.matmul(ps_bcast[:, :], ohT[:, j, :], enc_tab[:, :], start=True, stop=True)\
                  .then_inc(enc_bcast, 1)

            def transpose_x(s, j):
                n = tile_no(s, j)
                if j % 4 == 0:
                    pe.wait_ge(x_loaded[j // 4], 16 * (s + 1))
                if j >= 1 or later(s):
                    pe.wait_ge(x_T_copied, n)
                for c in range(HC):
                    last = nc.tensor.transpose(ps_xT[:, c * P:(c + 1) * P],
                                               x_in[:, j, c * P:(c + 1) * P], ident)
                last.then_inc(x_T, 1)

            def score(s, j):
                n = tile_no(s, j)
                pe.wait_ge(x_T_copied, n + 1)
                if j == 0 and later(s):
                    pe.wait_ge(route, route_at(s - 1, "scores_copied"))
                for c in range(HC):
                    last = nc.tensor.matmul(ps_sc[:, j, :], xT[:, j % 2, c * P:(c + 1) * P], gates[:, c, :],
                                            start=(c == 0), stop=(c == HC - 1))
                last.then_inc(scored, 1)

            def score_enc(s):
                pe.wait_ge(route, route_at(s, "enc_copied"))
                for b in range(2):
                    for c in range(HC):
                        last = nc.tensor.matmul(ps_es[:, b, :],
                                                enc_now[:, 4 * b + c:4 * b + c + 1].to_broadcast([P, P]),
                                                gates[:, c, 0:E], start=(c == 0), stop=(c == HC - 1))
                last.then_inc(enc_scored, 1)

            def enc_to_rows(s):
                if on(s - 2, NG):
                    pe.wait_ge(oh_T_copied, 2 * (s - 2) + 1)
                if later(s):
                    pe.wait_ge(route, route_at(s - 1, "enc_table"))
                pe.wait_ge(enc_split, len(ENC) * (s + 1))
                for c in range(HC):
                    for b in range(2):
                        last = nc.tensor.matmul(ps_enc[:, c * P:(c + 1) * P],
                                                enc_lhs[:, 4 * b + c, :, :].rearrange("p k b -> p (k b)"),
                                                ident_b[:, :], start=(b == 0), stop=(b == 1))
                last.then_inc(enc_rowed, 1)

            def rank_tokens(s):
                pe.wait_ge(route, route_at(s, "onehot"))
                for k in range(TS + 1):
                    last = nc.tensor.matmul(ps_rank.rearrange("p t e -> p (t e)"),
                                            (ones_b if k else before_b)[:, :],
                                            onehot_pad[:, TS - k:2 * TS + 1 - k, :].rearrange("p t e -> p (t e)"),
                                            start=(k == 0), stop=(k == TS))
                last.then_inc(ranked, 1)

            def transpose_onehot(g, h):
                pe.wait_ge(oh_set, 2 * g + h + 1)
                if h or later(g):
                    pe.wait_ge(oh_T_copied, 2 * g + h)
                if h == 1 and on(g + 2, NS):
                    pe.wait_ge(route, route_at(g + 2, "enc_table"))
                for k in range(4):
                    last = nc.tensor.transpose(ps_ohT[:, k, :], oh[:, k, :], ident_b[:, :])
                last.then_inc(oh_T, 1)

            def multiply(g, j):
                n = tile_no(g, j)
                pe.wait_ge(hi_set, n + 1)
                pe.wait_ge(lo_set, n + 1)
                if j >= 2 or later(g):
                    pe.wait_ge(res_set, n - 1)
                if j == 0:
                    pe.wait_ge(pick, pick_at(g, "expert"))
                    if isinstance(g, int) and g == 0:
                        pe.wait_ge(w_lo_set, HC * E)
                pe.wait_ge(tables_set, 1)
                e = pe.value_load(pick_expert[0:1, bass.ds(n, 1)], min_val=0, max_val=E - 1)
                k = 0
                for c in range(HC):
                    at = slice(c * H, (c + 1) * H)
                    xs = slice(c * P, (c + 1) * P)
                    for lhs, w in ((hiT, w_hi), (hiT, w_lo), (loT, w_hi)):
                        last = nc.tensor.matmul(ps_mm[:, j % 2, :], lhs[:, j % 2, xs],
                                                w[:, bass.ds(e, 1), at].rearrange("p a h -> p (a h)"),
                                                start=(k == 0), stop=(k == 3 * HC - 1))
                        k += 1
                last.then_inc(multiplied, 1)

            def step(t):
                for i in range(TS):
                    if on(ahead(t, i, 1)[0], NG):
                        transpose_ln(*ahead(t, i, 1))
                    if on(mixed(t, i)[0], NG):
                        spread_enc(*mixed(t, i))
                    if on(x_ahead(t, i)[0], NS):
                        transpose_x(*x_ahead(t, i))
                    if i in (1, 4) and on(t - 3, NG):
                        transpose_onehot(t - 3, i // 4)
                    if i == 1 and on(t - 1, NS):
                        score_enc(t - 1)
                    if i == 3 and on(t - 1, NS):
                        enc_to_rows(t - 1)
                        rank_tokens(t - 1)
                    if on(t - 4, NG):
                        multiply(t - 4, i)
                    for e, c in prepared(t, i):
                        transpose_weights(e, c)
                    if on(t, NS):
                        score(t, i)

            transpose_x(0, 0)
            for t in range(5):
                step(t)
            with pe.Fori(5, NS - 1) as t:
                step(t)
            for t in range(NS - 1, NG + 4):
                step(t)

        @block.vector
        def _(dve):
            tt, ts, cp = nc.vector.tensor_tensor, nc.vector.tensor_scalar, nc.vector.tensor_copy
            stt, reduce = nc.vector.scalar_tensor_tensor, nc.vector.tensor_reduce

            nc.vector.memset(g_rows[:, :], 0.0).then_inc(rows_clear, 1)
            nc.vector.memset(eps[:, :], EPS)
            nc.vector.memset(gates[:, :, E + 1:E + 2], 1.0)
            nc.vector.memset(ones_b[:, :], 1.0)
            nc.vector.memset(onehot_pad[:, :, :], 0.0)
            nc.vector.memset(enc_tab[:, :], 0.0)
            nc.vector.memset(done[:, :], 0.0)
            nc.vector.memset(ids_mix[:, :], 0)
            nc.vector.memset(enc_parts[:, :, 3:4], 0.0)
            dve.wait_ge(const_in, 16)
            cp(ident_b[:, :], table("ident"))
            cp(before_b[:, :], table("before"))
            cp(one31_b[:, :], table("one_at_31"))
            cp(batch_of_col_b[:, :], table("batch_of_col"))
            cp(counts[:, :], table("queue_start"))
            cp(next_ids[:, :], table("first_ids")).then_inc(tables_set, 1)
            dve.wait_ge(tables_set, 1)

            dve.wait_ge(gate_in, 32)
            reduce(g_sum[:, :], g_rows[:, :], AX.X, ALU.add).then_inc(gate_chain, 1)
            dve.wait_ge(gate_chain, 1)
            ts(g_sum[:, :], g_sum[:, :], -1.0 / H, None, ALU.mult).then_inc(gate_chain, 1)
            dve.wait_ge(gate_chain, 2)
            ts(g_rows[:, :], g_rows[:, :], g_sum[:, :], None, ALU.add).then_inc(gate_chain, 1)
            dve.wait_ge(gate_T, 1)
            cp(gates[:, :, 0:E + 1], ps_lnT[:, :].rearrange("p (c k) -> p c k", c=HC)[:, :, 0:E + 1])\
                .then_inc(gate_chain, 1)

            dve.wait_ge(small_in, 32)

            def weights_scale(e):
                col = slice(e, e + 1)
                dve.wait_ge(w_in[e % 2], 16 * (e // 2 + 1))
                reduce(w_max[:, col], w_stage[e % 2][:, :, :], AX.XY, ALU.max, apply_absolute_value=True)\
                    .then_inc(w_maxed, 1)
                dve.wait_ge(w_allmax, e + 1)
                ts(w_exp[:, col], w_amax[:, col].bitcast(I32), 23, None, ALU.logical_shift_right)\
                    .then_inc(w_chain, 1)
                dve.wait_ge(w_chain, 6 * e + 1)
                ts(w_exp[:, col], w_exp[:, col], W_TOP + LN_SHIFT + 1, None, ALU.max).then_inc(w_chain, 1)
                dve.wait_ge(w_chain, 6 * e + 2)
                ts(w_exp2[:, col], w_exp[:, col], -1.0, W_TOP + 254.0, ALU.mult, ALU.add).then_inc(w_chain, 1)
                dve.wait_ge(w_chain, 6 * e + 3)
                ts(w_exp[:, col], w_exp[:, col], float(W_TOP + LN_SHIFT), None, ALU.subtract)\
                    .then_inc(w_chain, 1)
                dve.wait_ge(w_chain, 6 * e + 4)
                ts(w_scale[:, col], w_exp2[:, col], 23, None, ALU.logical_shift_left).then_inc(w_chain, 1)
                ts(w_unscale[:, col], w_exp[:, col], 23, None, ALU.logical_shift_left).then_inc(w_chain, 1)

            def split_low(e, c):
                at = slice(c * H, (c + 1) * H)
                dve.wait_ge(w_chain, 6 * (e + 1))
                dve.wait_ge(w_hi_set, HC * e + c + 1)
                stt(w_lo[:, e, at], ps_mm[:, c % 2, :], w_scale[:, e:e + 1].bitcast(FP32), w_hi[:, e, at],
                    ALU.mult, ALU.subtract).then_inc(w_lo_set, 1)

            def routed(s, *names):
                dve.wait_ge(route, max(route_at(0, name) for name in names) + s * len(ROUTE))

            def route_slot0(s, gap):
                if gap == 0:
                    dve.wait_ge(scored, tile_no(s, TS))
                    cp(sc[:, :, :], ps_sc).then_inc(route, 1)
                    dve.wait_ge(ctx_dotted, tile_no(s, TS))
                    if later(s):
                        dve.wait_ge(enc_scored, s)
                        dve.wait_ge(enc_split, len(ENC) * s)
                    cp(enc_now[:, :], enc_col[:, :]).then_inc(route, 1)
                if gap == 1:
                    routed(s, "scores_copied")
                    stt(st_diff[:, :], sc[:, :, E + 1], float(SHIFT_OF) / H, x_shift[:, :],
                        ALU.mult, ALU.subtract).then_inc(route, 1)
                if gap == 2:
                    routed(s, "diff")
                    stt(st_diff2[:, :], st_diff[:, :], 1.0 / SHIFT_OF ** 2, st_diff[:, :],
                        ALU.mult, ALU.mult).then_inc(route, 1)
                if gap == 3:
                    routed(s, "diff2")
                    dve.wait_ge(x_squared, tile_no(s, TS))
                    stt(st_var[:, :], x_ss[:, :], 1.0 / H / SHIFT_OF ** 2, st_diff2[:, :],
                        ALU.mult, ALU.subtract).then_inc(route, 1)

            def route_slot1(s, gap):
                if gap == 3:
                    dve.wait_ge(enc_scored, s + 1)
                    tt(full_sc[:, :, :].rearrange("p (b j) e -> p b j e", b=2),
                       sc[:, :, 0:E].rearrange("p (b j) e -> p b j e", b=2),
                       ps_es.unsqueeze(2).to_broadcast([P, 2, 4, E]), ALU.add).then_inc(route, 1)
                if gap == 4:
                    routed(s, "scores")
                    reduce(best[:, :], full_sc[:, :, :], AX.X, ALU.max).then_inc(route, 1)
                if gap == 5:
                    routed(s, "best")
                    tt(is_best[:, :, :], full_sc[:, :, :], best[:, :].unsqueeze(2).to_broadcast([P, TS, E]),
                       ALU.is_ge).then_inc(route, 1)

            def route_slot2(s, gap):
                if gap == 0:
                    routed(s, "is_best")
                    tt(key[:, :, :], is_best[:, :, :],
                       table("first_key").unsqueeze(1).to_broadcast([P, TS, E]), ALU.mult).then_inc(route, 1)
                if gap == 1:
                    routed(s, "key")
                    reduce(best_key[:, :], key[:, :, :], AX.X, ALU.max).then_inc(route, 1)
                if gap == 2:
                    routed(s, "best_key")
                    if later(s):
                        dve.wait_ge(ranked, s)
                    tt(onehot, key[:, :, :], best_key[:, :].unsqueeze(2).to_broadcast([P, TS, E]),
                       ALU.is_equal).then_inc(route, 1)
                if gap == 3:
                    dve.wait_ge(std1_set, s + 1)
                    nc.vector.reciprocal(st_rstd[:, :], st_std[:, :]).then_inc(route, 1)
                if gap == 4:
                    routed(s, "rstd")
                    tt(st_d[:, :], sc[:, :, E], st_rstd[:, :], ALU.mult).then_inc(route, 1)

            def route_slot3(s, gap):
                if gap == 0:
                    routed(s, "d_scaled")
                    if later(s):
                        dve.wait_ge(queued, 16 * TS * s)
                    ts(payload[:, :, 1].bitcast(FP32), st_d[:, :], bias[:, :], None, ALU.add).then_inc(route, 1)
                    cp(payload[:, :, 0], next_ids[:, :]).then_inc(route, 1)
                if gap == 1:
                    routed(s, "payload")
                    ts(next_ids[:, :], next_ids[:, :], float(STEP_TOKENS), None, ALU.add).then_inc(route, 1)
                    dve.wait_ge(ranked, s + 1)
                    tt(rank[:, :, :], ps_rank[:, 0:TS, :], counts[:, :].unsqueeze(1).to_broadcast([P, TS, E]),
                       ALU.add).then_inc(route, 1)
                if gap == 2:
                    routed(s, "rank")
                    tt(rank_own[:, :, :], rank[:, :, :], onehot, ALU.mult).then_inc(route, 1)
                    tt(counts[:, :], counts[:, :], ps_rank[:, TS, :], ALU.add).then_inc(route, 1)
                if gap == 3:
                    routed(s, "rank_own")
                    reduce(entry_f[:, :], rank_own[:, :, :], AX.X, ALU.add).then_inc(route, 1)
                if gap == 4:
                    dve.wait_ge(enc_rowed, s + 1)
                    if on(s - 2, NG):
                        dve.wait_ge(enc_bcast, tile_no(s - 2, 2))
                    tt(enc_tab[:, :], enc_tab[:, :], ps_enc[:, :], ALU.add).then_inc(route, 1)
                if gap == 5:
                    routed(s, "entry_f")
                    cp(entry[:, :], entry_f[:, :]).then_inc(route, 1)

            def picked(g, name):
                dve.wait_ge(pick, pick_at(g, name))

            def spread(ap):
                return ap.unsqueeze(1).to_broadcast([P, TS, E])

            def pick_slot4(g, gap, all_routed):
                if gap == 0:
                    if not isinstance(g, int) or g + 1 < NS:
                        dve.wait_ge(route, route_at(g + 1, "counts"))
                    tt(full_i[:, :], counts[:, :], table("ceil_add" if all_routed else "floor_add"), ALU.add)\
                        .then_inc(pick, 1)
                    picked(g, "full_i")
                    ts(full[:, :], full_i[:, :], 7, None, ALU.logical_shift_right).then_inc(pick, 1)
                if gap == 1:
                    picked(g, "full")
                    tt(avail[:, :], full[:, :], done[:, :], ALU.subtract).then_inc(pick, 1)
                    picked(g, "avail")
                    tt(pre_t[:, :, :], avail[:, :].unsqueeze(1).to_broadcast([P, E, E]),
                       table("up_to").rearrange("p (a b) -> p a b", a=E), ALU.mult).then_inc(pick, 1)
                if gap == 2:
                    picked(g, "prefix_terms")
                    reduce(prefix[:, :], pre_t[:, :, :], AX.X, ALU.add).then_inc(pick, 1)
                if gap == 3:
                    picked(g, "prefix")
                    tt(passed[:, :, :], spread(prefix[:, :]),
                       table("pick").unsqueeze(2).to_broadcast([P, TS, E]), ALU.is_le).then_inc(pick, 1)
                    tt(start0[:, :], full[:, :], prefix[:, :], ALU.subtract).then_inc(pick, 1)
                if gap == 4:
                    picked(g, "start0")
                    reduce(expert_f[:, :], passed[:, :, :], AX.X, ALU.add).then_inc(pick, 1)
                    stt(start1[:, :], start0[:, :], float(P), table("queue_from_dummy"), ALU.mult, ALU.add)\
                        .then_inc(pick, 1)
                if gap == 5:
                    picked(g, "start1")
                    tt(chosen[:, :, :], spread(table("expert")),
                       expert_f[:, :].unsqueeze(2).to_broadcast([P, TS, E]), ALU.is_equal).then_inc(pick, 1)
                    picked(g, "chosen")
                    tt(start_t[:, :, :], chosen[:, :, :], spread(start1[:, :]), ALU.mult).then_inc(pick, 1)

            def pick_slot5(g, gap):
                here = bass.ds(tile_no(g, 0), TS)
                if gap == 0:
                    picked(g, "start_terms")
                    reduce(start_f[:, :], start_t[:, :, :], AX.X, ALU.add).then_inc(pick, 1)
                    picked(g, "start_f")
                    tt(pick_entry[:, here], start_f[:, :], table("pick_entry"), ALU.add).then_inc(pick, 1)
                if gap == 1:
                    ts(pick_expert[:, here], expert_f[:, :], float(E - 1), None, ALU.min).then_inc(pick, 1)
                    reduce(taken[:, :], chosen[:, :, :].rearrange("p i e -> p e i"), AX.X, ALU.add)\
                        .then_inc(pick, 1)
                if gap == 2:
                    picked(g, "taken")
                    tt(done[:, :], done[:, :], taken[:, :], ALU.add).then_inc(pick, 1)

            def scale_slot7(g, gap):
                here = bass.ds(tile_no(g, 0), TS)
                if gap == 1:
                    if later(g):
                        dve.wait_ge(scale, scale_at(g - 1, "scale_terms"))
                    tt(is_expert[:, :, :], spread(table("expert")),
                       pick_expert[:, here].unsqueeze(2).to_broadcast([P, TS, E]), ALU.is_equal)\
                        .then_inc(scale, 1)
                if gap == 2:
                    dve.wait_ge(scale, scale_at(g, "is_expert"))
                    if isinstance(g, int) and g == 0:
                        dve.wait_ge(w_chain, 6 * E)
                    tt(scale_t[:, :, :], is_expert[:, :, :], spread(w_unscale[:, :].bitcast(FP32)), ALU.mult)\
                        .then_inc(scale, 1)
                if gap == 3:
                    dve.wait_ge(scale, scale_at(g, "scale_terms"))
                    reduce(pick_scale[:, here], scale_t[:, :, :], AX.X, ALU.add).then_inc(scale, 1)

            def stats_done(g, h, name):
                dve.wait_ge(stats, half_at(STATS, g, h, name))

            def x1_stats(g, h):
                at = slice(4 * h, 4 * h + 4)
                dve.wait_ge(std2_set, 2 * g + h + 1)
                nc.vector.reciprocal(x1_rstd[:, at], x1_std[:, at]).then_inc(stats, 1)
                if later(g):
                    dve.wait_ge(base_set, tile_no(g - 1, 4 * h + 4))
                    dve.wait_ge(ln2_set, tile_no(g - 1, 4 * h + 4))
                stats_done(g, h, "rstd")
                ts(ln_scale[:, at], x1_rstd[:, at], float(1 << LN_SHIFT), None, ALU.mult).then_inc(stats, 1)
                stt(ln_bias[:, at], x1_nmean[:, at], float(1 << LN_SHIFT), x1_rstd[:, at], ALU.mult, ALU.mult)\
                    .then_inc(stats, 1)
                ts(base_scale[:, at], x1_rstd[:, at], 1.0, None, ALU.add).then_inc(stats, 1)
                tt(base_bias[:, at], x1_nmean[:, at], x1_rstd[:, at], ALU.mult).then_inc(stats, 1)

            def keep_for_scatter(g, h):
                at = slice(4 * h, 4 * h + 4)
                if on(g - 2, NG):
                    for k in range(4):
                        dve.wait_ge(stored[k], 16 * (2 * (g - 2) + h + 1))
                if later(g):
                    dve.wait_ge(keep, half_at(KEEP, g - 1, h, "ids_mix"))
                cp(ids_out[:, at], ids_mix[:, at]).then_inc(keep, 1 if on(g, NG) else 2)

            def keep_from_meta(g, h):
                at = slice(4 * h, 4 * h + 4)
                for k in range(4):
                    dve.wait_ge(meta_in[4 * h + k], 16 * (g + 1))
                dve.wait_ge(keep, half_at(KEEP, g, h, "ids_out"))
                cp(ids_mix[:, at], meta[:, at, 0].bitcast(U32)).then_inc(keep, 1)

            def onehot_batches(g, h):
                for k in range(4):
                    dve.wait_ge(meta_in[4 * h + k], 16 * (g + 1))
                at = slice(4 * h, 4 * h + 4)
                ts(batch_no[:, at], meta[:, at, 0], S.bit_length() - 1, None, ALU.logical_shift_right)\
                    .then_inc(batch_set, 1)
                dve.wait_ge(batch_set, 2 * g + h + 1)
                if h or later(g):
                    dve.wait_ge(oh_T, 2 * g + h)
                for k in range(4):
                    last = ts(oh[:, k, :], batch_of_col_b[:, :], batch_no[:, 4 * h + k:4 * h + k + 1], None,
                              ALU.is_equal)
                last.then_inc(oh_set, 1)

            def mix(g, j):
                n = tile_no(g, j)
                dve.wait_ge(enc_bcast, n + 1)
                dve.wait_ge(got[j], 16 * (g + 1))
                if later(g):
                    dve.wait_ge(base_set, tile_no(g - 1, j + 1))
                    dve.wait_ge(ln2_set, tile_no(g - 1, j + 1))
                    dve.wait_ge(squared, tile_no(g - 1, j + 1))
                stt(x1[:, j, :], x_got[:, j, :], meta[:, j, 1:2].bitcast(FP32), ps_bcast[:, :],
                    ALU.add, ALU.add, accum_out=x1_sum[:, j:j + 1]).then_inc(x1_set, 1)

            def negative_mean(g, j):
                dve.wait_ge(x1_set, tile_no(g, j) + 1)
                ts(x1_nmean[:, j:j + 1], x1_sum[:, j:j + 1], -1.0 / H, None, ALU.mult).then_inc(nmean_set, 1)

            def low(g, j):
                n = tile_no(g, j)
                dve.wait_ge(hi_set, n + 1)
                if j >= 2 or later(g):
                    dve.wait_ge(multiplied, n - 1)
                tt(loT[:, j % 2, :], ps_lnT[:, :], hiT[:, j % 2, :], ALU.subtract).then_inc(lo_set, 1)

            def finish(g, j):
                n = tile_no(g, j)
                dve.wait_ge(multiplied, n + 1)
                dve.wait_ge(base_set, n + 1)
                if j == 0:
                    dve.wait_ge(scale, scale_at(g, "scale"))
                if j >= 4 or later(g):
                    dve.wait_ge(stored[j % 4], 16 * (2 * g + j // 4))
                stt(res[:, j % 4, :], ps_mm[:, j % 2, :], pick_scale[:, bass.ds(n, 1)], base[:, j % 4, :],
                    ALU.mult, ALU.add).then_inc(res_set, 1)

            def dot_ctx(s, j):
                if j % 4 == 0:
                    dve.wait_ge(c_loaded[j // 4], 16 * (s + 1))
                if later(s):
                    dve.wait_ge(route, route_at(s - 1, "enc_copied"))
                stt(c_in[:, j, :], c_in[:, j, :], 1.0, w_enc[:, :], ALU.mult, ALU.mult,
                    accum_out=enc_col[:, j:j + 1]).then_inc(ctx_dotted, 1)

            def shift_x(s, h):
                at = slice(4 * h, 4 * h + 4)
                dve.wait_ge(x_loaded[h], 16 * (s + 1))
                if later(s):
                    dve.wait_ge(route, route_at(s - 1, "diff"))
                    dve.wait_ge(x_squared, tile_no(s - 1, 4 * h + 4))
                reduce(x_shift[:, at], x_in[:, at, 0:SHIFT_OF], AX.X, ALU.add).then_inc(x_shifted, 1)

            def step(t):
                def between(i, gap):
                    if gap == 1 and i == 2 and on(t - 4, NG):
                        x1_stats(t - 4, 1)
                    if gap == 1 and i == 6 and on(t - 3, NG):
                        x1_stats(t - 3, 0)
                    if i == 7 and on(t - 3, NG):
                        scale_slot7(t - 3, gap)
                    if on(t - 1, NS):
                        if i < 4:
                            (route_slot0, route_slot1, route_slot2, route_slot3)[i](t - 1, gap)
                    if on(t - 2, NG):
                        if i == 4:
                            pick_slot4(t - 2, gap, isinstance(t, int) and t >= NS)
                        if i == 5:
                            pick_slot5(t - 2, gap)

                for i in range(TS):
                    if i in (0, 4) and on(t - 3, NG + 1):
                        keep_for_scatter(t - 3, i // 4)
                    if i in (1, 4) and on(t - 3, NG):
                        keep_from_meta(t - 3, i // 4)
                        onehot_batches(t - 3, i // 4)
                    if isinstance(t, int) and t < E // 2 and i in (2, 4):
                        weights_scale(2 * t + (i - 2) // 2)
                    between(i, 0)
                    if on(ahead(t, i, -1)[0], NG):
                        finish(*ahead(t, i, -1))
                    between(i, 1)
                    if on(mixed(t, i)[0], NG):
                        mix(*mixed(t, i))
                    between(i, 2)
                    if on(t, NS):
                        dot_ctx(t, i)
                    between(i, 3)
                    if on(mixed(t, i)[0], NG):
                        negative_mean(*mixed(t, i))
                    if on(ahead(t, i, 1)[0], NG):
                        low(*ahead(t, i, 1))
                    between(i, 4)
                    if i in (0, 4) and on(t, NS):
                        shift_x(t, i // 4)
                    between(i, 5)
                    for e, c in prepared(t, i):
                        split_low(e, c)

            for t in range(5):
                step(t)
            with dve.Fori(5, NS) as t:
                step(t)
            for t in range(NS, NG + 4):
                step(t)
            finish(NG - 1, TS - 1)


_INS = ['x', 'ctx_1024', 'L0_xattn_mlp_weight', 'L0_xattn_mlp_bias', 'L0_ffn_gate_w', 'L0_ffn_expert_w']


def kernel(**inputs):
    import numpy as _np
    import concourse.bacc as _bacc
    from concourse import mybir as _mybir
    from concourse.bass_utils import run_bass_kernel_spmd as _run

    nc = _bacc.Bacc("TRN2", target_bir_lowering=False, num_devices=1)
    const, cols = constants()
    arrays, args = {}, []
    for name, a in [(n, inputs[n]) for n in _INS] + [("const", const)]:
        a = _np.ascontiguousarray(a)
        arrays[f"in_{name}"] = a
        args.append(nc.dram_tensor(f"in_{name}", a.shape, _mybir.dt.from_np(a.dtype), kind="ExternalInput").ap())
    out = nc.dram_tensor("out_0", (B, S, H), _mybir.dt.float32, kind="ExternalOutput").ap()
    build(nc, *args, cols, out)
    r = _run(nc, [arrays], core_ids=[0])
    return r.results[0]["out_0"]
```

```python
import concourse.bass as bass
from concourse import mybir
from contextlib import ExitStack
import numpy as np

FP32 = mybir.dt.float32
FP16 = mybir.dt.float16
BF16 = mybir.dt.bfloat16
I32 = mybir.dt.int32
U32 = mybir.dt.uint32
ALU = mybir.AluOpType
ACT = mybir.ActivationFunctionType
AX = mybir.AxisListType

P = 128
B, S, H, E = 32, 512, 512, 8
N = B * S
HC = H // P
TS = 8
STEP_TOKENS = TS * P
NS = N // STEP_TOKENS
TILES = (N + E * (P - 1)) // P
NG = -(-TILES // TS)
QUEUE = N + P
DUMMY = E * QUEUE
ENTRIES = DUMMY + TS * P
NO_TOKEN = 1 << 20
EPS = 1e-5
FILL_COLUMNS = 64
SHIFT_OF = 32
W_TOP = 13
LN_SHIFT = 8
SPLIT_SLOT = (3, 5, 8, 11, 14, 17, 20, 22)
assert ENTRIES % P == 0


def constants():
    p = np.arange(P)[:, None]
    e = np.arange(E)
    j = np.arange(TS)
    c = np.arange(P)
    parts = {
        "ident": (c[None] == p),
        "before": (p < c[None]),
        "batch_of_col": np.where(c < 3 * B, c % B, -1)[None],
        "up_to": np.tril(np.ones((E, E))).reshape(1, -1),
        "first_key": (E - e)[None],
        "expert": e[None],
        "pick": j[None],
        "queue_start": (e * QUEUE)[None],
        "floor_add": (-e * QUEUE)[None],
        "ceil_add": (P - 1 - e * QUEUE)[None],
        "queue_from_dummy": (e * QUEUE - DUMMY)[None],
        "pick_entry": (j * P + DUMMY)[None],
        "first_ids": j[None] * P + p,
    }
    at, cols, out = 0, {}, []
    for name, a in parts.items():
        a = np.broadcast_to(np.asarray(a, np.float32), (P, np.asarray(a).shape[1]))
        cols[name] = (at, at + a.shape[1])
        at += a.shape[1]
        out.append(a)
    return np.ascontiguousarray(np.concatenate(out, 1)), cols


ROUTE = ["scores_copied", "enc_copied", "diff", "enc_terms", "diff2", "enc_sums", "var", "scores", "best", "is_best",
         "key", "best_key", "onehot", "rstd", "d_scaled", "payload_d", "payload", "next_ids",
         "rank", "rank_own", "counts", "entry_f", "entry", "enc_table"]
ENC = ["hi", "rest", "mid", "parts", "columns"]
PICK = ["full_i", "full", "avail", "prefix_terms", "prefix", "passed", "start0", "expert_f", "start1",
        "chosen", "start_terms", "start_f", "entry", "expert", "taken", "done"]
SCALE = ["is_expert", "scale_terms", "scale"]
STATS = ["rstd", "ln_scale", "ln_bias", "base_scale", "base_bias"]
KEEP = ["ids_out", "ids_mix"]


def build(nc, x, ctx, mlp_weight, mlp_bias, gate_w, expert_w, const, cols, out):
    x_rows = x.rearrange("b s h -> (b s) h")
    out_rows = out.rearrange("b s h -> (b s) h")
    queue = nc.dram_tensor("queue", [ENTRIES, 2], I32, kind="Internal").ap()

    with ExitStack() as stack:
        def sb(name, shape, dt):
            return stack.enter_context(nc.sbuf_tensor(name, shape, dt))

        def pb(name, shape, dt):
            return stack.enter_context(nc.psum_tensor(name, shape, dt))

        def sem(name):
            return stack.enter_context(nc.semaphore(name))

        cst = sb("cst", [P, const.shape[1]], FP32)

        def table(name):
            return cst[:, cols[name][0]:cols[name][1]]
        ident_b = sb("ident_b", [P, P], BF16)
        before_b = sb("before_b", [P, P], BF16)
        ones_b = sb("ones_b", [P, P], BF16)
        ones = sb("ones", [P, P], FP32)
        batch_of_col_b = sb("batch_of_col_b", [P, P], BF16)
        w_hi = sb("w_hi", [P, E, HC * H], FP16)
        w_lo = sb("w_lo", [P, E, HC * H], FP16)
        w_enc = sb("w_enc", [P, H], FP32)
        bias = sb("bias", [P, 1], FP32)
        eps = sb("eps", [P, 1], FP32)
        g_rows = sb("g_rows", [P, H], FP32)
        g_sum = sb("g_sum", [P, 1], FP32)
        gates = sb("gates", [P, HC, FILL_COLUMNS], FP32)
        w_sum = sb("w_sum", [P, E], FP32)
        w_bound = sb("w_bound", [P, E], FP32)
        w_exp = sb("w_exp", [P, E], I32)
        w_exp2 = sb("w_exp2", [P, E], I32)
        w_scale = sb("w_scale", [P, E], I32)
        w_unscale = sb("w_unscale", [P, E], I32)
        x_in = sb("x_in", [P, TS, H], FP32)
        c_in = sb("c_in", [P, TS, H], FP32)
        xT = sb("xT", [P, 2, HC * P], FP32)
        junk_x = sb("junk_x", [P, H], FP32)
        junk_x1 = sb("junk_x1", [P, H], FP32)
        enc_col = sb("enc_col", [P, TS], FP32)
        x_shift = sb("x_shift", [P, TS], FP32)
        x_ss = sb("x_ss", [P, TS], FP32)
        sc = sb("sc", [P, TS, E + 2], FP32)
        enc_now = sb("enc_now", [P, TS], FP32)
        enc_parts = sb("enc_parts", [P, TS, 4], BF16)
        es_terms = sb("es_terms", [P, 2, E, HC], FP32)
        es_sums = sb("es_sums", [P, 2, E], FP32)
        enc_rest = sb("enc_rest", [P, TS], FP32)
        enc_lhs = sb("enc_lhs", [P, HC, 4, B], BF16)
        zeros_b = sb("zeros_b", [P, HC, 4, 2], BF16)
        enc_tab = sb("enc_tab", [P, H], BF16)
        st_diff = sb("st_diff", [P, TS], FP32)
        st_diff2 = sb("st_diff2", [P, TS], FP32)
        st_var = sb("st_var", [P, TS], FP32)
        st_std = sb("st_std", [P, TS], FP32)
        st_rstd = sb("st_rstd", [P, TS], FP32)
        st_d = sb("st_d", [P, TS], FP32)
        full_sc = sb("full_sc", [P, TS, E], FP32)
        best = sb("best", [P, TS], FP32)
        is_best = sb("is_best", [P, TS, E], FP32)
        key = sb("key", [P, TS, E], FP32)
        best_key = sb("best_key", [P, TS], FP32)
        onehot_pad = sb("onehot_pad", [P, 2 * TS + 1, E], BF16)
        onehot = onehot_pad[:, TS:2 * TS, :]
        counts = sb("counts", [P, E], FP32)
        rank = sb("rank", [P, TS, E], FP32)
        rank_own = sb("rank_own", [P, TS, E], FP32)
        entry_f = sb("entry_f", [P, TS], FP32)
        entry = sb("entry", [P, TS], U32)
        next_ids = sb("next_ids", [P, TS], FP32)
        payload = sb("payload", [P, TS, 2], I32)
        full_i = sb("full_i", [P, E], I32)
        full = sb("full", [P, E], I32)
        avail = sb("avail", [P, E], FP32)
        done = sb("done", [P, E], FP32)
        pre_t = sb("pre_t", [P, E, E], FP32)
        prefix = sb("prefix", [P, E], FP32)
        passed = sb("passed", [P, TS, E], FP32)
        expert_f = sb("expert_f", [P, TS], FP32)
        chosen = sb("chosen", [P, TS, E], FP32)
        start0 = sb("start0", [P, E], FP32)
        start1 = sb("start1", [P, E], FP32)
        start_t = sb("start_t", [P, TS, E], FP32)
        start_f = sb("start_f", [P, TS], FP32)
        taken = sb("taken", [P, E], FP32)
        is_expert = sb("is_expert", [P, TS, E], FP32)
        scale_t = sb("scale_t", [P, TS, E], FP32)
        pick_entry = sb("pick_entry", [P, NG * TS], I32)
        pick_expert = sb("pick_expert", [P, NG * TS], I32)
        pick_scale = sb("pick_scale", [P, NG * TS], FP32)
        meta = sb("meta", [P, TS, 2], I32)
        batch_no = sb("batch_no", [P, TS], I32)
        oh = sb("oh", [P, TS // 2, P], BF16)
        ohT = sb("ohT", [P, TS, P], BF16)
        x_got = sb("x_got", [P, TS, H], FP32)
        x1 = sb("x1", [P, TS, H], FP32)
        x1_sum = sb("x1_sum", [P, TS], FP32)
        x1_nmean = sb("x1_nmean", [P, TS], FP32)
        x1_ss = sb("x1_ss", [P, TS], FP32)
        x1_std = sb("x1_std", [P, TS], FP32)
        x1_rstd = sb("x1_rstd", [P, TS], FP32)
        ln_scale = sb("ln_scale", [P, TS], FP32)
        ln_bias = sb("ln_bias", [P, TS], FP32)
        base_scale = sb("base_scale", [P, TS], FP32)
        base_bias = sb("base_bias", [P, TS], FP32)
        ids_mix = sb("ids_mix", [P, TS], U32)
        ids_out = sb("ids_out", [P, TS], U32)
        ln2 = sb("ln2", [P, 2, H], FP32)
        hiT = sb("hiT", [P, 2, HC * P], FP16)
        loT = sb("loT", [P, 2, HC * P], FP16)
        base = sb("base", [P, 4, H], FP32)
        res = sb("res", [P, 4, H], FP32)

        w_stage = (base[:, :, :], res[:, :, :], x1[:, 0:4, :], x1[:, 4:8, :])

        ps_xT = pb("ps_xT", [P, HC * P], FP32)
        ps_scores = pb("ps_scores", [P, 512], FP32)
        ps_rows = pb("ps_rows", [P, 512], FP32)
        ps_route = pb("ps_route", [P, 512], FP32)
        ps_bcast = pb("ps_bcast", [P, H], FP32)
        ps_lnT = pb("ps_lnT", [P, HC * P], FP32)
        ps_mm = pb("ps_mm", [P, 2, H], FP32)
        ps_w = (ps_mm[:, 0, :], ps_mm[:, 1, :], ps_bcast[:, :], ps_lnT[:, :])
        ps_sc = ps_scores[:, 0:TS * FILL_COLUMNS].rearrange("p (t e) -> p t e", e=FILL_COLUMNS)
        ps_enc = ps_rows[:, 0:H]
        ps_ohT = ps_rows[:, 0:4 * P // 2].bitcast(BF16).rearrange("p (t c) -> p t c", c=P)
        ps_es = ps_route[:, 0:2 * E].rearrange("p (b e) -> p b e", e=E)
        ps_rank = ps_route[:, 128:128 + (TS + 1) * E].rearrange("p (t e) -> p t e", e=E)

        const_in = sem("const_in")
        small_in = sem("small_in")
        gate_in = sem("gate_in")
        queue_fill = sem("queue_fill")
        queue_filled = sem("queue_filled")
        tables_set = sem("tables_set")
        rows_clear = sem("rows_clear")
        gate_chain = sem("gate_chain")
        gate_T = sem("gate_T")
        w_in = [sem(f"w_in{k}") for k in range(len(w_stage))]
        w_summed = sem("w_summed")
        w_bounded = sem("w_bounded")
        w_chain = sem("w_chain")
        w_T = sem("w_T")
        w_hi_set = sem("w_hi_set")
        w_lo_set = sem("w_lo_set")
        x_loaded = [sem(f"x_loaded{k}") for k in range(2)]
        c_loaded = [sem(f"c_loaded{k}") for k in range(2)]
        x_T = sem("x_T")
        x_T_copied = sem("x_T_copied")
        scored = sem("scored")
        ctx_dotted = sem("ctx_dotted")
        x_shifted = sem("x_shifted")
        x_squared = sem("x_squared")
        route = sem("route")
        enc_split = sem("enc_split")
        enc_scored = sem("enc_scored")
        enc_rowed = sem("enc_rowed")
        ranked = sem("ranked")
        std1_set = sem("std1_set")
        queued = sem("queued")
        pool_waited = sem("pool_waited")
        sp_waited = sem("sp_waited")
        pick = sem("pick")
        scale = sem("scale")
        meta_in = [sem(f"meta_in{j}") for j in range(TS)]
        got = [sem(f"got{j}") for j in range(TS)]
        keep = sem("keep")
        batch_set = sem("batch_set")
        oh_set = sem("oh_set")
        oh_T = sem("oh_T")
        oh_T_copied = sem("oh_T_copied")
        enc_bcast = sem("enc_bcast")
        x1_set = sem("x1_set")
        nmean_set = sem("nmean_set")
        squared = sem("squared")
        std2_set = sem("std2_set")
        stats = sem("stats")
        ln2_set = sem("ln2_set")
        ln_T = sem("ln_T")
        hi_set = sem("hi_set")
        lo_set = sem("lo_set")
        base_set = sem("base_set")
        multiplied = sem("multiplied")
        res_set = sem("res_set")
        stored = [sem(f"stored{k}") for k in range(4)]

        def route_at(s, name):
            return s * len(ROUTE) + (ROUTE.index(name) + 1)

        def pick_at(g, name):
            return g * len(PICK) + (PICK.index(name) + 1)

        def scale_at(g, name):
            return g * len(SCALE) + (SCALE.index(name) + 1)

        def half_at(chain, g, h, name):
            return (2 * g + h) * len(chain) + (chain.index(name) + 1)

        def tile_no(g, j):
            return g * TS + j

        def mixed(t, i):
            return t - 3 + (i - 2) // TS, (i - 2) % TS

        def ahead(t, i, k):
            return t - 4 + (i + k) // TS, (i + k) % TS

        def x_ahead(t, i):
            return t + (i + 1) // TS, (i + 1) % TS

        def prepared(t, i):
            if not isinstance(t, int):
                return []
            return [(e, 2 * k + c) for e in range(E) for k in range(2) for c in range(2)
                    if SPLIT_SLOT[e] + k == t * TS + i]

        def experts_at(t, i, before):
            return [e for e in range(E) if isinstance(t, int) and max(SPLIT_SLOT[e] - before, 1) == t * TS + i]

        def on(k, count):
            return not isinstance(k, int) or 0 <= k < count

        def taken_on(t, i, k):
            g, j = ahead(t, i, k)
            return not isinstance(g, int) or 0 <= tile_no(g, j) < TILES

        def later(k):
            return not isinstance(k, int) or k > 0

        block = stack.enter_context(nc.Block())

        @block.sync
        def _(sp):
            sp.dma_start(cst[:, :], const).then_inc(const_in, 16)
            sp.dma_start(x_in[:, 0:4, :], x[0].rearrange("(j p) h -> p j h", p=P)).then_inc(x_loaded[0], 16)
            sp.wait_ge(rows_clear, 1)
            sp.dma_start(g_rows[0:E, :], gate_w).then_inc(gate_in, 16)
            sp.dma_start(g_rows[E:E + 1, :], mlp_weight[:, H:2 * H]).then_inc(gate_in, 16)
            sp.dma_start(w_enc[:, :], mlp_weight[:, 0:H].partition_broadcast(P)).then_inc(small_in, 16)
            sp.dma_start(bias[:, :], mlp_bias.partition_broadcast(P)).then_inc(small_in, 16)

            def alone(semaphore, value):
                sp.wait_ge(semaphore, value)
                sp.sem_inc(sp_waited, 1)

            def load_one(dst, dram, arrived, src, h):
                sp.dma_start(dst[:, 4 * h:4 * h + 4, :],
                             dram[bass.ds(src, 1), :, :].rearrange("a (j p) h -> p (a j) h", p=P))\
                  .then_inc(arrived[h], 16)

            def load_half(s, h):
                if later(s):
                    alone(x_T, tile_no(s - 1, 4 * h + 4))
                    alone(x_squared, tile_no(s - 1, 4 * h + 4))
                    alone(ctx_dotted, tile_no(s - 1, 4 * h + 4))
                src = 2 * s + h
                load_one(x_in, x, x_loaded, src, h)
                load_one(c_in, ctx, c_loaded, src, h)

            def load_weights(e):
                k = len(w_stage)
                if e >= k:
                    alone(w_lo_set, HC * (e - k + 1))
                sp.dma_start(w_stage[e % k], expert_w[e].rearrange("(c p) h -> p c h", p=P))\
                  .then_inc(w_in[e % k], 16)

            def fill_queues():
                sp.wait_ge(queue_fill, 1)
                sp.dma_start(queue.rearrange("(p n) c -> p (n c)", p=P),
                             x_got[:, :, :].rearrange("p t h -> p (t h)").bitcast(I32)[:, 0:2 * ENTRIES // P])\
                  .then_inc(queue_filled, 16)

            def find_meta(g, j):
                return sp.value_load(pick_entry[0:1, bass.ds(tile_no(g, j), 1)], min_val=0, max_val=ENTRIES - P)

            def read_meta(g, j, at):
                if later(g):
                    if j in (0, 4):
                        alone(keep, half_at(KEEP, g - 1, j // 4, "ids_mix"))
                        alone(batch_set, 2 * (g - 1) + j // 4 + 1)
                    alone(x1_set, tile_no(g - 1, j + 1))
                sp.dma_start(meta[:, j, :], queue[bass.ds(at, P), :]).then_inc(meta_in[j], 16)

            for h in range(2):
                if h == 1:
                    load_one(x_in, x, x_loaded, h, h)
                load_weights(h)
                load_one(c_in, ctx, c_loaded, h, h)
            load_weights(2)

            def step(t):
                s, g = t, t - 2
                first = t if isinstance(t, int) else None
                if first == 1:
                    load_weights(5)
                if on(s + 1, NS):
                    load_half(s + 1, 0)
                if first == 0:
                    load_weights(3)
                    fill_queues()
                    load_weights(4)
                if first == 1:
                    load_weights(6)
                if on(g, NG):
                    alone(pick, pick_at(g, "entry"))
                    places = [find_meta(g, j) for j in range(TS)]
                    routed = g + 1 if not isinstance(g, int) else min(g + 1, NS - 1)
                    alone(queued, 16 * TS * (routed + 1))
                    for j in range(6):
                        read_meta(g, j, places[j])
                if on(s + 1, NS):
                    load_half(s + 1, 1)
                if first == 1:
                    load_weights(7)
                if on(g, NG):
                    for j in range(6, TS):
                        read_meta(g, j, places[j])

            for t in range(5):
                step(t)
            with sp.Fori(5, NS - 1) as t:
                step(t)
            for t in range(NS - 1, NG + 4):
                step(t)
            for k in range(4):
                sp.wait_ge(stored[k], 16 * ((TILES - k + 3) // 4))

        @block.gpsimd
        def _(pool):
            nc.gpsimd.memset(x_got[:, :, :].bitcast(I32), NO_TOKEN).then_inc(queue_fill, 1)
            pool.wait_ge(queue_fill, 1)
            pool.wait_ge(tables_set, 4)

            def widest(e):
                pool.wait_ge(w_summed, e + 1)
                nc.gpsimd.partition_all_reduce(w_bound[:, e:e + 1], w_sum[:, e:e + 1], P,
                                               bass.bass_isa.ReduceOp.absmax).then_inc(w_bounded, 1)

            def plain(value, semaphore):
                pool.wait_ge(semaphore, value)
                pool.sem_inc(pool_waited, 1)

            def enqueue(s, j):
                if isinstance(s, int) and s == 0 and j == 0:
                    pool.wait_ge(queue_filled, 16)
                plain(route_at(s, "entry"), route)
                pool.indirect_dma_start(queue, bass.IndirectOffsetOnAxis(ap=entry[:, j:j + 1], axis=0),
                                        payload[:, j, :], None,
                                        bounds_check=ENTRIES - 1, oob_is_err=False).then_inc(queued, 16)

            def gather(g, j):
                if later(g):
                    plain(tile_no(g - 1, j + 1), x1_set)
                plain(16 * (g + 1), meta_in[j])
                pool.indirect_dma_start(x_got[:, j, :], None, x_rows,
                                        bass.IndirectOffsetOnAxis(ap=meta[:, j, 0:1].bitcast(U32), axis=0),
                                        bounds_check=N - 1, oob_is_err=False).then_inc(got[j], 16)

            def scatter(g, j):
                plain(half_at(KEEP, g + 1, j // 4, "ids_out"), keep)
                plain(tile_no(g, j + 1), res_set)
                pool.indirect_dma_start(out_rows, bass.IndirectOffsetOnAxis(ap=ids_out[:, j:j + 1], axis=0),
                                        res[:, j % 4, :], None,
                                        bounds_check=N - 1, oob_is_err=False).then_inc(stored[j % 4], 16)

            def enc_at(s, name):
                return s * len(ENC) + (ENC.index(name) + 1)

            def split_enc(s):
                tt, cp = nc.gpsimd.tensor_tensor, nc.gpsimd.tensor_copy
                if later(s):
                    plain(s, enc_rowed)
                plain(route_at(s, "enc_copied"), route)
                cp(enc_parts[:, :, 0], enc_now[:, :]).then_inc(enc_split, 1)
                plain(enc_at(s, "hi"), enc_split)
                tt(enc_rest[:, :], enc_now[:, :], enc_parts[:, :, 0], ALU.subtract).then_inc(enc_split, 1)
                plain(enc_at(s, "rest"), enc_split)
                cp(enc_parts[:, :, 1], enc_rest[:, :]).then_inc(enc_split, 1)
                plain(enc_at(s, "mid"), enc_split)
                tt(enc_parts[:, :, 2], enc_rest[:, :], enc_parts[:, :, 1], ALU.subtract).then_inc(enc_split, 1)
                plain(enc_at(s, "parts"), enc_split)
                if later(s):
                    cp(enc_lhs[:, :, :, bass.ds(2 * s - 2, 2)], zeros_b[:, :, :, :])
                last = cp(enc_lhs[:, :, :, bass.ds(2 * s, 2)],
                          enc_parts[:, :, :].rearrange("p (b c) k -> p c k b", b=2))
                last.then_inc(enc_split, 1)

            enqueues = {3: (0, 1), 4: (2, 3, 4), 5: (5, 6, 7)}
            gathers = {7: (0, 1, 2), 8: (3, 4), 9: (5,), 10: (6,), 11: (7,)}

            def step(t):
                for i in range(TS):
                    for j in gathers.get(i + TS, ()):
                        if on(t - 3, NG):
                            gather(t - 3, j)
                    if taken_on(t, i, -1):
                        scatter(*ahead(t, i, -1))
                    if i == 0 and on(t - 1, NS):
                        split_enc(t - 1)
                    for e in experts_at(t, i, 3):
                        widest(e)
                    if on(t - 1, NS):
                        for j in enqueues.get(i, ()):
                            enqueue(t - 1, j)
                    for j in gathers.get(i, ()):
                        if on(t - 2, NG):
                            gather(t - 2, j)

            for t in range(5):
                step(t)
            with pool.Fori(5, NS) as t:
                step(t)
            for t in range(NS, NG + 4):
                step(t)

        @block.scalar
        def _(act):
            act.wait_ge(const_in, 16)
            for dst, name in ((ident_b, "ident"), (before_b, "before"), (batch_of_col_b, "batch_of_col")):
                nc.scalar.activation(dst[:, :], table(name), ACT.Copy).then_inc(tables_set, 1)
            act.wait_ge(tables_set, 4)

            def weights_sum(e):
                act.wait_ge(w_in[e % len(w_stage)], 16 * (e // len(w_stage) + 1))
                nc.scalar.activation(w_lo[:, e, :], w_stage[e % len(w_stage)].rearrange("p c h -> p (c h)"), ACT.Abs,
                                     accum_out=w_sum[:, e:e + 1]).then_inc(w_summed, 1)

            def split_high(e, c):
                act.wait_ge(w_T, HC * e + c + 1)
                act.wait_ge(w_chain, 6 * (e + 1))
                nc.scalar.activation(w_hi[:, e, c * H:(c + 1) * H], ps_w[c], ACT.Copy,
                                     scale=w_scale[:, e:e + 1].bitcast(FP32)).then_inc(w_hi_set, 1)

            def std_x1(g, h):
                act.wait_ge(squared, tile_no(g, 4 * h + 4))
                if later(g):
                    act.wait_ge(stats, half_at(STATS, g - 1, h, "rstd"))
                nc.scalar.activation(x1_std[:, 4 * h:4 * h + 4], x1_ss[:, 4 * h:4 * h + 4], ACT.Sqrt,
                                     bias=eps[:, :], scale=1.0 / H).then_inc(std2_set, 1)

            def std_x(s):
                act.wait_ge(route, route_at(s, "var"))
                nc.scalar.activation(st_std[:, :], st_var[:, :], ACT.Sqrt, bias=eps[:, :]).then_inc(std1_set, 1)

            def copy_xT(s, j):
                n = tile_no(s, j)
                act.wait_ge(x_T, n + 1)
                if j >= 2 or later(s):
                    act.wait_ge(scored, n - 1)
                nc.scalar.activation(xT[:, j % 2, :], ps_xT[:, :], ACT.Copy).then_inc(x_T_copied, 1)

            def square_x(s, j):
                act.wait_ge(x_shifted, 2 * s + j // 4 + 1)
                if later(s) and j == 0:
                    act.wait_ge(route, route_at(s - 1, "var"))
                if later(s) or j > 0:
                    act.wait_ge(x_squared, tile_no(s, j))
                nc.scalar.activation(junk_x[:, :], x_in[:, j, :], ACT.Square, bias=x_shift[:, j:j + 1],
                                     scale=-float(SHIFT_OF), accum_out=x_ss[:, j:j + 1]).then_inc(x_squared, 1)

            def square(g, j):
                n = tile_no(g, j)
                act.wait_ge(nmean_set, n + 1)
                if later(g):
                    act.wait_ge(std2_set, 2 * (g - 1) + j // 4 + 1)
                if j >= 1 or later(g):
                    act.wait_ge(squared, n)
                nc.scalar.activation(junk_x1[:, :], x1[:, j, :], ACT.Square, bias=x1_nmean[:, j:j + 1],
                                     accum_out=x1_ss[:, j:j + 1]).then_inc(squared, 1)

            def high(g, j):
                n = tile_no(g, j)
                act.wait_ge(ln_T, n + 1)
                if j >= 2 or later(g):
                    act.wait_ge(multiplied, n - 1)
                nc.scalar.activation(hiT[:, j % 2, :], ps_lnT[:, :], ACT.Copy).then_inc(hi_set, 1)

            def make_base(g, j):
                n = tile_no(g, j)
                act.wait_ge(stats, half_at(STATS, g, j // 4, "base_bias"))
                if j >= 4 or later(g):
                    act.wait_ge(res_set, n - 3)
                nc.scalar.activation(base[:, j % 4, :], x1[:, j, :], ACT.Identity,
                                     bias=base_bias[:, j:j + 1], scale=base_scale[:, j:j + 1])\
                  .then_inc(base_set, 1)

            def normalise(g, j):
                n = tile_no(g, j)
                act.wait_ge(stats, half_at(STATS, g, j // 4, "base_bias"))
                if j >= 2 or later(g):
                    act.wait_ge(ln_T, n - 1)
                nc.scalar.activation(ln2[:, j % 2, :], x1[:, j, :], ACT.Identity,
                                     bias=ln_bias[:, j:j + 1], scale=ln_scale[:, j:j + 1])\
                  .then_inc(ln2_set, 1)

            def copy_ohT(g, h):
                act.wait_ge(oh_T, 2 * g + h + 1)
                if later(g):
                    act.wait_ge(enc_bcast, tile_no(g - 1, 4 * h + 4))
                nc.scalar.activation(ohT[:, 4 * h:4 * h + 4, :], ps_ohT[:, :, :], ACT.Copy)\
                  .then_inc(oh_T_copied, 1)

            def step(t):
                for i in range(TS):
                    if i == 2 and on(t - 4, NG):
                        std_x1(t - 4, 1)
                    if i == 6 and on(t - 3, NG):
                        std_x1(t - 3, 0)
                    if taken_on(t, i, 1):
                        high(*ahead(t, i, 1))
                    if on(x_ahead(t, i)[0], NS):
                        copy_xT(*x_ahead(t, i))
                    if i in (1, 5) and on(t - 3, NG):
                        copy_ohT(t - 3, i // 4)
                    if i == 1 and on(t - 1, NS):
                        std_x(t - 1)
                    for e, c in prepared(t, i):
                        split_high(e, c)
                    if taken_on(t, i, 1):
                        make_base(*ahead(t, i, 1))
                    if taken_on(t, i, 2):
                        normalise(*ahead(t, i, 2))
                    if on(mixed(t, i)[0], NG):
                        square(*mixed(t, i))
                    if on(t, NS):
                        square_x(t, i)
                    for e in experts_at(t, i, 3):
                        weights_sum(e)

            copy_xT(0, 0)
            for t in range(5):
                step(t)
            with act.Fori(5, NS - 1) as t:
                step(t)
            for t in range(NS - 1, NG + 4):
                step(t)

        @block.tensor
        def _(pe):
            pe.wait_ge(const_in, 16)
            ident = table("ident")

            def transpose_weights(e, c):
                n = HC * e + c
                pe.wait_ge(w_in[e % len(w_stage)], 16 * (e // len(w_stage) + 1))
                if n >= HC:
                    pe.wait_ge(w_lo_set, n - HC + 1)
                for f in range(HC):
                    last = nc.tensor.transpose(ps_w[c][:, f * P:(f + 1) * P],
                                               w_stage[e % len(w_stage)][:, f, c * P:(c + 1) * P], ident)
                last.then_inc(w_T, 1)

            def transpose_ln(g, j):
                n = tile_no(g, j)
                pe.wait_ge(ln2_set, n + 1)
                if j >= 1 or later(g):
                    pe.wait_ge(lo_set, n)
                for c in range(HC):
                    last = nc.tensor.transpose(ps_lnT[:, c * P:(c + 1) * P],
                                               ln2[:, j % 2, c * P:(c + 1) * P], ident)
                last.then_inc(ln_T, 1)

            def spread_enc(g, j):
                n = tile_no(g, j)
                if j % 4 == 0:
                    pe.wait_ge(oh_T_copied, 2 * g + j // 4 + 1)
                if j >= 1 or later(g):
                    pe.wait_ge(x1_set, n)
                if isinstance(g, int) and g == 0 and j == 0:
                    pe.wait_ge(w_lo_set, HC * E)
                if j in (0, 2):
                    rows = g + 1 + j // 2
                    pe.wait_ge(route, route_at(min(rows, NS - 1) if isinstance(g, int) else rows, "enc_table"))
                nc.tensor.matmul(ps_bcast[:, :], ohT[:, j, :], enc_tab[:, :], start=True, stop=True)\
                  .then_inc(enc_bcast, 1)

            def transpose_x(s, j):
                n = tile_no(s, j)
                if j % 4 == 0:
                    pe.wait_ge(x_loaded[j // 4], 16 * (s + 1))
                if j >= 1 or later(s):
                    pe.wait_ge(x_T_copied, n)
                for c in range(HC):
                    last = nc.tensor.transpose(ps_xT[:, c * P:(c + 1) * P],
                                               x_in[:, j, c * P:(c + 1) * P], ident)
                last.then_inc(x_T, 1)

            def score(s, j):
                n = tile_no(s, j)
                pe.wait_ge(x_T_copied, n + 1)
                if j == 0 and later(s):
                    pe.wait_ge(route, route_at(s - 1, "scores_copied"))
                columns = slice(0, FILL_COLUMNS if isinstance(s, int) and s < 4 else E + 2)
                for c in range(HC):
                    last = nc.tensor.matmul(ps_sc[:, j, columns], xT[:, j % 2, c * P:(c + 1) * P],
                                            gates[:, c, columns],
                                            start=(c == 0), stop=(c == HC - 1))
                last.then_inc(scored, 1)

            def score_enc(s):
                pe.wait_ge(route, route_at(s, "enc_sums"))
                nc.tensor.matmul(ps_es.rearrange("p b e -> p (b e)"), ones[:, :],
                                 es_sums[:, :, :].rearrange("p b e -> p (b e)"), start=True, stop=True)\
                  .then_inc(enc_scored, 1)

            def enc_to_rows(s):
                if on(s - 2, NG):
                    pe.wait_ge(oh_T_copied, 2 * (s - 2) + 1)
                if later(s):
                    pe.wait_ge(route, route_at(s - 1, "enc_table"))
                pe.wait_ge(enc_split, len(ENC) * (s + 1))
                for c in range(HC):
                    last = nc.tensor.matmul(ps_enc[:, c * P:(c + 1) * P],
                                            enc_lhs[:, c, :, :].rearrange("p k b -> p (k b)"),
                                            ident_b[:, :], start=True, stop=True)
                last.then_inc(enc_rowed, 1)

            def rank_tokens(s):
                pe.wait_ge(route, route_at(s, "onehot"))
                for k in range(TS + 1):
                    last = nc.tensor.matmul(ps_rank.rearrange("p t e -> p (t e)"),
                                            (ones_b if k else before_b)[:, :],
                                            onehot_pad[:, TS - k:2 * TS + 1 - k, :].rearrange("p t e -> p (t e)"),
                                            start=(k == 0), stop=(k == TS))
                last.then_inc(ranked, 1)

            def transpose_onehot(g, h):
                pe.wait_ge(oh_set, 2 * g + h + 1)
                if h or later(g):
                    pe.wait_ge(oh_T_copied, 2 * g + h)
                if h == 1 and on(g + 2, NS):
                    pe.wait_ge(route, route_at(g + 2, "enc_table"))
                for k in range(4):
                    last = nc.tensor.transpose(ps_ohT[:, k, :], oh[:, k, :], ident_b[:, :])
                last.then_inc(oh_T, 1)

            def find_expert(g, j):
                if j == 0:
                    pe.wait_ge(pick, pick_at(g, "expert"))
                pe.wait_ge(tables_set, 4)
                return pe.value_load(pick_expert[0:1, bass.ds(tile_no(g, j), 1)], min_val=0, max_val=E - 1)

            def multiply(g, j, e):
                n = tile_no(g, j)
                pe.wait_ge(hi_set, n + 1)
                pe.wait_ge(lo_set, n + 1)
                if j >= 2 or later(g):
                    pe.wait_ge(res_set, n - 1)
                k = 0
                for c in range(HC):
                    at = slice(c * H, (c + 1) * H)
                    xs = slice(c * P, (c + 1) * P)
                    for lhs, w in ((hiT, w_hi), (hiT, w_lo), (loT, w_hi)):
                        last = nc.tensor.matmul(ps_mm[:, j % 2, :], lhs[:, j % 2, xs],
                                                w[:, bass.ds(e, 1), at].rearrange("p a h -> p (a h)"),
                                                start=(k == 0), stop=(k == 3 * HC - 1))
                        k += 1
                last.then_inc(multiplied, 1)

            def step(t):
                for i in range(TS):
                    if taken_on(t, i, 0):
                        e = find_expert(t - 4, i)
                    if taken_on(t, i, 1):
                        transpose_ln(*ahead(t, i, 1))
                    if on(mixed(t, i)[0], NG):
                        spread_enc(*mixed(t, i))
                    if on(x_ahead(t, i)[0], NS):
                        transpose_x(*x_ahead(t, i))
                    if i in (1, 5) and on(t - 3, NG):
                        transpose_onehot(t - 3, i // 4)
                    if i == 1 and on(t - 1, NS):
                        score_enc(t - 1)
                    if i == 3 and on(t - 1, NS):
                        enc_to_rows(t - 1)
                    if taken_on(t, i, 0):
                        multiply(t - 4, i, e)
                    if i == 2 and on(t - 1, NS):
                        rank_tokens(t - 1)
                    for e, c in prepared(t, i):
                        transpose_weights(e, c)
                    if on(t, NS):
                        score(t, i)

            transpose_x(0, 0)
            pe.wait_ge(gate_chain, 3)
            for c in range(HC):
                last = nc.tensor.transpose(ps_lnT[:, c * P:(c + 1) * P], g_rows[:, c * P:(c + 1) * P], ident)
            last.then_inc(gate_T, 1)
            pe.wait_ge(gate_chain, 4)
            for t in range(5):
                step(t)
            with pe.Fori(5, NS - 1) as t:
                step(t)
            for t in range(NS - 1, NG + 4):
                step(t)

        @block.vector
        def _(dve):
            tt, ts, cp = nc.vector.tensor_tensor, nc.vector.tensor_scalar, nc.vector.tensor_copy
            stt, reduce = nc.vector.scalar_tensor_tensor, nc.vector.tensor_reduce

            nc.vector.memset(g_rows[:, :], 0.0).then_inc(rows_clear, 1)
            nc.vector.memset(eps[:, :], EPS)
            nc.vector.memset(gates[:, :, E + 2:], 0.0)
            nc.vector.memset(gates[:, :, E + 1:E + 2], 1.0)
            nc.vector.memset(ones_b[:, :], 1.0)
            nc.vector.memset(ones[:, :], 1.0)
            nc.vector.memset(onehot_pad[:, :, :], 0.0)
            nc.vector.memset(enc_tab[:, :], 0.0)
            nc.vector.memset(done[:, :], 0.0)
            nc.vector.memset(ids_mix[:, :], 0)
            nc.vector.memset(enc_parts[:, :, 3:4], 0.0)
            nc.vector.memset(enc_lhs[:, :, :, :], 0.0)
            nc.vector.memset(zeros_b[:, :, :, :], 0.0)
            dve.wait_ge(const_in, 16)
            cp(counts[:, :], table("queue_start"))
            cp(next_ids[:, :], table("first_ids")).then_inc(tables_set, 1)
            dve.wait_ge(tables_set, 4)

            dve.wait_ge(gate_in, 32)
            reduce(g_sum[:, :], g_rows[:, :], AX.X, ALU.add).then_inc(gate_chain, 1)
            dve.wait_ge(gate_chain, 1)
            ts(g_sum[:, :], g_sum[:, :], -1.0 / H, None, ALU.mult).then_inc(gate_chain, 1)
            dve.wait_ge(gate_chain, 2)
            ts(g_rows[:, :], g_rows[:, :], g_sum[:, :], None, ALU.add).then_inc(gate_chain, 1)
            dve.wait_ge(gate_T, 1)
            cp(gates[:, :, 0:E + 1], ps_lnT[:, :].rearrange("p (c k) -> p c k", c=HC)[:, :, 0:E + 1])\
                .then_inc(gate_chain, 1)

            dve.wait_ge(small_in, 32)

            def weights_scale(e):
                col = slice(e, e + 1)
                dve.wait_ge(w_bounded, e + 1)
                ts(w_exp[:, col], w_bound[:, col].bitcast(I32), 23, None, ALU.logical_shift_right)\
                    .then_inc(w_chain, 1)
                dve.wait_ge(w_chain, 6 * e + 1)
                ts(w_exp[:, col], w_exp[:, col], W_TOP + LN_SHIFT + 1, None, ALU.max).then_inc(w_chain, 1)
                dve.wait_ge(w_chain, 6 * e + 2)
                ts(w_exp2[:, col], w_exp[:, col], -1.0, W_TOP + 254.0, ALU.mult, ALU.add).then_inc(w_chain, 1)
                dve.wait_ge(w_chain, 6 * e + 3)
                ts(w_exp[:, col], w_exp[:, col], float(W_TOP + LN_SHIFT), None, ALU.subtract)\
                    .then_inc(w_chain, 1)
                dve.wait_ge(w_chain, 6 * e + 4)
                ts(w_scale[:, col], w_exp2[:, col], 23, None, ALU.logical_shift_left).then_inc(w_chain, 1)
                ts(w_unscale[:, col], w_exp[:, col], 23, None, ALU.logical_shift_left).then_inc(w_chain, 1)

            def split_low(e, c):
                at = slice(c * H, (c + 1) * H)
                dve.wait_ge(w_chain, 6 * (e + 1))
                dve.wait_ge(w_hi_set, HC * e + c + 1)
                stt(w_lo[:, e, at], ps_w[c], w_scale[:, e:e + 1].bitcast(FP32), w_hi[:, e, at],
                    ALU.mult, ALU.subtract).then_inc(w_lo_set, 1)

            def routed(s, *names):
                dve.wait_ge(route, max(route_at(0, name) for name in names) + s * len(ROUTE))

            def route_slot0(s, gap):
                if gap == 0:
                    dve.wait_ge(scored, tile_no(s, TS))
                    cp(sc[:, :, :], ps_sc[:, :, 0:E + 2]).then_inc(route, 1)
                    dve.wait_ge(ctx_dotted, tile_no(s, TS))
                    if later(s):
                        dve.wait_ge(enc_scored, s)
                        dve.wait_ge(enc_split, len(ENC) * s)
                    cp(enc_now[:, :], enc_col[:, :]).then_inc(route, 1)
                if gap == 1:
                    routed(s, "scores_copied")
                    stt(st_diff[:, :], sc[:, :, E + 1], float(SHIFT_OF) / H, x_shift[:, :],
                        ALU.mult, ALU.subtract).then_inc(route, 1)
                    routed(s, "enc_copied")
                    tt(es_terms[:, :, :, :],
                       gates[:, :, 0:E].rearrange("p c e -> p e c").unsqueeze(1).to_broadcast([P, 2, E, HC]),
                       enc_now[:, :].rearrange("p (b c) -> p b c", b=2).unsqueeze(2).to_broadcast([P, 2, E, HC]),
                       ALU.mult).then_inc(route, 1)
                if gap == 2:
                    routed(s, "diff")
                    stt(st_diff2[:, :], st_diff[:, :], 1.0 / SHIFT_OF ** 2, st_diff[:, :],
                        ALU.mult, ALU.mult).then_inc(route, 1)
                    routed(s, "enc_terms")
                    reduce(es_sums[:, :, :], es_terms[:, :, :, :], AX.X, ALU.add).then_inc(route, 1)
                if gap == 3:
                    routed(s, "diff2")
                    dve.wait_ge(x_squared, tile_no(s, TS))
                    stt(st_var[:, :], x_ss[:, :], 1.0 / H / SHIFT_OF ** 2, st_diff2[:, :],
                        ALU.mult, ALU.subtract).then_inc(route, 1)

            def route_slot1(s, gap):
                if gap == 1:
                    dve.wait_ge(enc_scored, s + 1)
                    tt(full_sc[:, :, :].rearrange("p (b j) e -> p b j e", b=2),
                       sc[:, :, 0:E].rearrange("p (b j) e -> p b j e", b=2),
                       ps_es.unsqueeze(2).to_broadcast([P, 2, 4, E]), ALU.add).then_inc(route, 1)
                if gap == 2:
                    routed(s, "scores")
                    reduce(best[:, :], full_sc[:, :, :], AX.X, ALU.max).then_inc(route, 1)
                if gap == 3:
                    routed(s, "best")
                    tt(is_best[:, :, :], full_sc[:, :, :], best[:, :].unsqueeze(2).to_broadcast([P, TS, E]),
                       ALU.is_ge).then_inc(route, 1)
                if gap == 4:
                    routed(s, "is_best")
                    tt(key[:, :, :], is_best[:, :, :],
                       table("first_key").unsqueeze(1).to_broadcast([P, TS, E]), ALU.mult).then_inc(route, 1)
                if gap == 5:
                    routed(s, "key")
                    reduce(best_key[:, :], key[:, :, :], AX.X, ALU.max).then_inc(route, 1)

            def route_slot2(s, gap):
                if gap == 0:
                    routed(s, "best_key")
                    if later(s):
                        dve.wait_ge(ranked, s)
                    tt(onehot, key[:, :, :], best_key[:, :].unsqueeze(2).to_broadcast([P, TS, E]),
                       ALU.is_equal).then_inc(route, 1)
                if gap == 1:
                    dve.wait_ge(std1_set, s + 1)
                    nc.vector.reciprocal(st_rstd[:, :], st_std[:, :]).then_inc(route, 1)
                if gap == 2:
                    routed(s, "rstd")
                    tt(st_d[:, :], sc[:, :, E], st_rstd[:, :], ALU.mult).then_inc(route, 1)
                if gap == 3:
                    routed(s, "d_scaled")
                    if later(s):
                        dve.wait_ge(queued, 16 * TS * s)
                    ts(payload[:, :, 1].bitcast(FP32), st_d[:, :], bias[:, :], None, ALU.add).then_inc(route, 1)
                    cp(payload[:, :, 0], next_ids[:, :]).then_inc(route, 1)
                if gap == 4:
                    routed(s, "payload")
                    ts(next_ids[:, :], next_ids[:, :], float(STEP_TOKENS), None, ALU.add).then_inc(route, 1)

            def route_slot3(s, gap):
                if gap == 0:
                    dve.wait_ge(ranked, s + 1)
                    tt(rank[:, :, :], ps_rank[:, 0:TS, :], counts[:, :].unsqueeze(1).to_broadcast([P, TS, E]),
                       ALU.add).then_inc(route, 1)
                if gap == 1:
                    routed(s, "rank")
                    tt(rank_own[:, :, :], rank[:, :, :], onehot, ALU.mult).then_inc(route, 1)
                    tt(counts[:, :], counts[:, :], ps_rank[:, TS, :], ALU.add).then_inc(route, 1)
                if gap == 2:
                    routed(s, "rank_own")
                    reduce(entry_f[:, :], rank_own[:, :, :], AX.X, ALU.add).then_inc(route, 1)
                if gap == 3:
                    routed(s, "entry_f")
                    cp(entry[:, :], entry_f[:, :]).then_inc(route, 1)
                if gap == 4:
                    dve.wait_ge(enc_rowed, s + 1)
                    if on(s - 2, NG):
                        dve.wait_ge(enc_bcast, tile_no(s - 2, 2))
                    tt(enc_tab[:, :], enc_tab[:, :], ps_enc[:, :], ALU.add).then_inc(route, 1)

            def picked(g, name):
                dve.wait_ge(pick, pick_at(g, name))

            def spread(ap):
                return ap.unsqueeze(1).to_broadcast([P, TS, E])

            def pick_slot4(g, gap, all_routed):
                if gap == 0:
                    if not isinstance(g, int) or g + 1 < NS:
                        dve.wait_ge(route, route_at(g + 1, "counts"))
                    tt(full_i[:, :], counts[:, :], table("ceil_add" if all_routed else "floor_add"), ALU.add)\
                        .then_inc(pick, 1)
                    picked(g, "full_i")
                    ts(full[:, :], full_i[:, :], 7, None, ALU.logical_shift_right).then_inc(pick, 1)
                if gap == 1:
                    picked(g, "full")
                    tt(avail[:, :], full[:, :], done[:, :], ALU.subtract).then_inc(pick, 1)
                    picked(g, "avail")
                    tt(pre_t[:, :, :], avail[:, :].unsqueeze(1).to_broadcast([P, E, E]),
                       table("up_to").rearrange("p (a b) -> p a b", a=E), ALU.mult).then_inc(pick, 1)
                if gap == 2:
                    picked(g, "prefix_terms")
                    reduce(prefix[:, :], pre_t[:, :, :], AX.X, ALU.add).then_inc(pick, 1)
                if gap == 3:
                    picked(g, "prefix")
                    tt(passed[:, :, :], spread(prefix[:, :]),
                       table("pick").unsqueeze(2).to_broadcast([P, TS, E]), ALU.is_le).then_inc(pick, 1)
                    tt(start0[:, :], full[:, :], prefix[:, :], ALU.subtract).then_inc(pick, 1)
                if gap == 4:
                    picked(g, "start0")
                    reduce(expert_f[:, :], passed[:, :, :], AX.X, ALU.add).then_inc(pick, 1)
                    stt(start1[:, :], start0[:, :], float(P), table("queue_from_dummy"), ALU.mult, ALU.add)\
                        .then_inc(pick, 1)
                if gap == 5:
                    picked(g, "start1")
                    tt(chosen[:, :, :], spread(table("expert")),
                       expert_f[:, :].unsqueeze(2).to_broadcast([P, TS, E]), ALU.is_equal).then_inc(pick, 1)
                    picked(g, "chosen")
                    tt(start_t[:, :, :], chosen[:, :, :], spread(start1[:, :]), ALU.mult).then_inc(pick, 1)

            def pick_slot5(g, gap):
                here = bass.ds(tile_no(g, 0), TS)
                if gap == 0:
                    picked(g, "start_terms")
                    reduce(start_f[:, :], start_t[:, :, :], AX.X, ALU.add).then_inc(pick, 1)
                    picked(g, "start_f")
                    tt(pick_entry[:, here], start_f[:, :], table("pick_entry"), ALU.add).then_inc(pick, 1)
                if gap == 1:
                    ts(pick_expert[:, here], expert_f[:, :], float(E - 1), None, ALU.min).then_inc(pick, 1)
                    reduce(taken[:, :], chosen[:, :, :].rearrange("p i e -> p e i"), AX.X, ALU.add)\
                        .then_inc(pick, 1)
                if gap == 2:
                    picked(g, "taken")
                    tt(done[:, :], done[:, :], taken[:, :], ALU.add).then_inc(pick, 1)

            def scale_slot7(g, gap):
                here = bass.ds(tile_no(g, 0), TS)
                if gap == 1:
                    if later(g):
                        dve.wait_ge(scale, scale_at(g - 1, "scale_terms"))
                    tt(is_expert[:, :, :], spread(table("expert")),
                       pick_expert[:, here].unsqueeze(2).to_broadcast([P, TS, E]), ALU.is_equal)\
                        .then_inc(scale, 1)
                if gap == 2:
                    dve.wait_ge(scale, scale_at(g, "is_expert"))
                    if isinstance(g, int) and g == 0:
                        dve.wait_ge(w_chain, 6 * E)
                    tt(scale_t[:, :, :], is_expert[:, :, :], spread(w_unscale[:, :].bitcast(FP32)), ALU.mult)\
                        .then_inc(scale, 1)
                if gap == 3:
                    dve.wait_ge(scale, scale_at(g, "scale_terms"))
                    reduce(pick_scale[:, here], scale_t[:, :, :], AX.X, ALU.add).then_inc(scale, 1)

            def stats_done(g, h, name):
                dve.wait_ge(stats, half_at(STATS, g, h, name))

            def x1_stats(g, h):
                at = slice(4 * h, 4 * h + 4)
                dve.wait_ge(std2_set, 2 * g + h + 1)
                nc.vector.reciprocal(x1_rstd[:, at], x1_std[:, at]).then_inc(stats, 1)
                if later(g):
                    dve.wait_ge(base_set, tile_no(g - 1, 4 * h + 4))
                    dve.wait_ge(ln2_set, tile_no(g - 1, 4 * h + 4))
                stats_done(g, h, "rstd")
                ts(ln_scale[:, at], x1_rstd[:, at], float(1 << LN_SHIFT), None, ALU.mult).then_inc(stats, 1)
                stt(ln_bias[:, at], x1_nmean[:, at], float(1 << LN_SHIFT), x1_rstd[:, at], ALU.mult, ALU.mult)\
                    .then_inc(stats, 1)
                ts(base_scale[:, at], x1_rstd[:, at], 1.0, None, ALU.add).then_inc(stats, 1)
                tt(base_bias[:, at], x1_nmean[:, at], x1_rstd[:, at], ALU.mult).then_inc(stats, 1)

            def keep_for_scatter(g, h):
                at = slice(4 * h, 4 * h + 4)
                if on(g - 2, NG):
                    for k in range(4):
                        dve.wait_ge(stored[k], 16 * (2 * (g - 2) + h + 1))
                if later(g):
                    dve.wait_ge(keep, half_at(KEEP, g - 1, h, "ids_mix"))
                cp(ids_out[:, at], ids_mix[:, at]).then_inc(keep, 1 if on(g, NG) else 2)

            def keep_from_meta(g, h):
                at = slice(4 * h, 4 * h + 4)
                for k in range(4):
                    dve.wait_ge(meta_in[4 * h + k], 16 * (g + 1))
                dve.wait_ge(keep, half_at(KEEP, g, h, "ids_out"))
                cp(ids_mix[:, at], meta[:, at, 0].bitcast(U32)).then_inc(keep, 1)

            def onehot_batches(g, h):
                for k in range(4):
                    dve.wait_ge(meta_in[4 * h + k], 16 * (g + 1))
                at = slice(4 * h, 4 * h + 4)
                ts(batch_no[:, at], meta[:, at, 0], S.bit_length() - 1, None, ALU.logical_shift_right)\
                    .then_inc(batch_set, 1)
                dve.wait_ge(batch_set, 2 * g + h + 1)
                if h or later(g):
                    dve.wait_ge(oh_T, 2 * g + h)
                for k in range(4):
                    last = ts(oh[:, k, :], batch_of_col_b[:, :], batch_no[:, 4 * h + k:4 * h + k + 1], None,
                              ALU.is_equal)
                last.then_inc(oh_set, 1)

            def mix(g, j):
                n = tile_no(g, j)
                dve.wait_ge(enc_bcast, n + 1)
                dve.wait_ge(got[j], 16 * (g + 1))
                if later(g):
                    dve.wait_ge(base_set, tile_no(g - 1, j + 1))
                    dve.wait_ge(ln2_set, tile_no(g - 1, j + 1))
                    dve.wait_ge(squared, tile_no(g - 1, j + 1))
                stt(x1[:, j, :], x_got[:, j, :], meta[:, j, 1:2].bitcast(FP32), ps_bcast[:, :],
                    ALU.add, ALU.add, accum_out=x1_sum[:, j:j + 1]).then_inc(x1_set, 1)

            def negative_mean(g, j):
                dve.wait_ge(x1_set, tile_no(g, j) + 1)
                ts(x1_nmean[:, j:j + 1], x1_sum[:, j:j + 1], -1.0 / H, None, ALU.mult).then_inc(nmean_set, 1)

            def low(g, j):
                n = tile_no(g, j)
                dve.wait_ge(hi_set, n + 1)
                if j >= 2 or later(g):
                    dve.wait_ge(multiplied, n - 1)
                tt(loT[:, j % 2, :], ps_lnT[:, :], hiT[:, j % 2, :], ALU.subtract).then_inc(lo_set, 1)

            def finish(g, j):
                n = tile_no(g, j)
                dve.wait_ge(multiplied, n + 1)
                dve.wait_ge(base_set, n + 1)
                if j == 0:
                    dve.wait_ge(scale, scale_at(g, "scale"))
                if j >= 4 or later(g):
                    dve.wait_ge(stored[j % 4], 16 * (2 * g + j // 4))
                stt(res[:, j % 4, :], ps_mm[:, j % 2, :], pick_scale[:, bass.ds(n, 1)], base[:, j % 4, :],
                    ALU.mult, ALU.add).then_inc(res_set, 1)

            def dot_ctx(s, j):
                if j % 4 == 0:
                    dve.wait_ge(c_loaded[j // 4], 16 * (s + 1))
                if later(s):
                    dve.wait_ge(route, route_at(s - 1, "enc_copied"))
                stt(c_in[:, j, :], c_in[:, j, :], 1.0, w_enc[:, :], ALU.mult, ALU.mult,
                    accum_out=enc_col[:, j:j + 1]).then_inc(ctx_dotted, 1)

            def shift_x(s, h):
                at = slice(4 * h, 4 * h + 4)
                dve.wait_ge(x_loaded[h], 16 * (s + 1))
                if later(s):
                    dve.wait_ge(route, route_at(s - 1, "diff"))
                    dve.wait_ge(x_squared, tile_no(s - 1, 4 * h + 4))
                reduce(x_shift[:, at], x_in[:, at, 0:SHIFT_OF], AX.X, ALU.add).then_inc(x_shifted, 1)

            def step(t):
                def between(i, gap):
                    if gap == 1 and i == 2 and on(t - 4, NG):
                        x1_stats(t - 4, 1)
                    if gap == 1 and i == 6 and on(t - 3, NG):
                        x1_stats(t - 3, 0)
                    if i == 7 and on(t - 3, NG):
                        scale_slot7(t - 3, gap)
                    if on(t - 1, NS):
                        if i < 4:
                            (route_slot0, route_slot1, route_slot2, route_slot3)[i](t - 1, gap)
                    if on(t - 2, NG):
                        if i == 4:
                            pick_slot4(t - 2, gap, isinstance(t, int) and t >= NS)
                        if i == 5:
                            pick_slot5(t - 2, gap)

                for i in range(TS):
                    if i in (0, 4) and on(t - 3, NG + 1):
                        keep_for_scatter(t - 3, i // 4)
                    if i in (1, 4) and on(t - 3, NG):
                        keep_from_meta(t - 3, i // 4)
                        onehot_batches(t - 3, i // 4)
                    between(i, 0)
                    if taken_on(t, i, -1):
                        finish(*ahead(t, i, -1))
                    between(i, 1)
                    if on(mixed(t, i)[0], NG):
                        mix(*mixed(t, i))
                    between(i, 2)
                    if i in (0, 3) and on(t, NS):
                        shift_x(t, i // 3)
                    if on(t, NS):
                        dot_ctx(t, i)
                    between(i, 3)
                    if on(mixed(t, i)[0], NG):
                        negative_mean(*mixed(t, i))
                    if taken_on(t, i, 1):
                        low(*ahead(t, i, 1))
                    between(i, 4)
                    between(i, 5)
                    for e in experts_at(t, i, 1):
                        weights_scale(e)
                    for e, c in prepared(t, i):
                        split_low(e, c)

            for t in range(5):
                step(t)
            with dve.Fori(5, NS) as t:
                step(t)
            for t in range(NS, NG + 4):
                step(t)


_INS = ['x', 'ctx_1024', 'L0_xattn_mlp_weight', 'L0_xattn_mlp_bias', 'L0_ffn_gate_w', 'L0_ffn_expert_w']


def kernel(**inputs):
    import numpy as _np
    import concourse.bacc as _bacc
    from concourse import mybir as _mybir
    from concourse.bass_utils import run_bass_kernel_spmd as _run

    nc = _bacc.Bacc("TRN2", target_bir_lowering=False, num_devices=1)
    const, cols = constants()
    arrays, args = {}, []
    for name, a in [(n, inputs[n]) for n in _INS] + [("const", const)]:
        a = _np.ascontiguousarray(a)
        arrays[f"in_{name}"] = a
        args.append(nc.dram_tensor(f"in_{name}", a.shape, _mybir.dt.from_np(a.dtype), kind="ExternalInput").ap())
    out = nc.dram_tensor("out_0", (B, S, H), _mybir.dt.float32, kind="ExternalOutput").ap()
    build(nc, *args, cols, out)
    r = _run(nc, [arrays], core_ids=[0])
    return r.results[0]["out_0"]
```
